# Optimizing a Trainium2 kernel written in Bass

```python
import numpy as np
import jax
import jax.numpy as jnp

def _softmax(x, axis=-1):
    return jax.nn.softmax(x, axis=axis)

def _gelu(x):
    return jax.nn.gelu(x, approximate=True)

def _silu(x):
    return jax.nn.silu(x)

def _sigmoid(x):
    return jax.nn.sigmoid(x)

def _layernorm(x, axis=-1, eps=1e-05):
    m = jnp.mean(x, axis=axis, keepdims=True)
    v = jnp.var(x, axis=axis, keepdims=True)
    return (x - m) / jnp.sqrt(v + eps)

def _scatter_add(tgt, idx, src, axis=0):
    return tgt.at[idx].add(src)

def _segment_sum(src, seg, n):
    return jax.ops.segment_sum(src, seg, n)
kernel_name = 'mk_seq_preln_d1_jaxref_r4_a9ee1f'

def setup_inputs(seed: int=0):
    np.random.seed(seed)
    _w = jnp.asarray

    def _L0_attn_setup():
        import jax, jax.numpy as jnp
        import numpy as np
        import math
        EMBED_DIM = 256
        NUM_HEADS = 8
        DEPTH = 12
        HEAD_DIM = EMBED_DIM // NUM_HEADS // 2
        LAMBDA_INIT = 0.8 - 0.6 * math.exp(-0.3 * DEPTH)
        EPS = 1e-08

        def _rotary(t):
            d = t.shape[-1]
            s = t.shape[1]
            inv_freq = 1.0 / 10000.0 ** (jnp.arange(0, d, 2, dtype=jnp.float32) / d)
            pos = jnp.arange(s, dtype=jnp.float32)
            freqs = pos[:, None] * inv_freq[None, :]
            freqs = jnp.repeat(freqs, 2, axis=-1)
            cos = jnp.cos(freqs)[None, :, None, :]
            sin = jnp.sin(freqs)[None, :, None, :]
            x = t.reshape(t.shape[:-1] + (d // 2, 2))
            x1, x2 = (x[..., 0], x[..., 1])
            rot = jnp.stack([-x2, x1], axis=-1).reshape(t.shape)
            return t * cos + rot * sin

        def _sdpa_over_heads(q, k, v):
            scores = jnp.einsum('bsnd,bsmd->bsnm', q, k) / HEAD_DIM ** 0.25
            aw = jax.nn.softmax(scores, axis=-1)
            return jnp.einsum('bsnm,bsme->bsne', aw, v)
        key = jax.random.key(seed)
        ks = jax.random.split(key, 10)
        E, H, D = (EMBED_DIM, NUM_HEADS, HEAD_DIM)
        scale = 1.0 / np.sqrt(E)
        return {'x': jax.random.normal(ks[0], (4, 1024, E), jnp.float32), 'Wq': jax.random.normal(ks[1], (E, E), jnp.float32) * scale, 'Wk': jax.random.normal(ks[2], (E, E), jnp.float32) * scale, 'Wv': jax.random.normal(ks[3], (E, E), jnp.float32) * scale, 'Wo': jax.random.normal(ks[4], (E, E), jnp.float32) * scale, 'lambda_q1': jax.random.normal(ks[5], (D,), jnp.float32) * 0.1, 'lambda_k1': jax.random.normal(ks[6], (D,), jnp.float32) * 0.1, 'lambda_q2': jax.random.normal(ks[7], (D,), jnp.float32) * 0.1, 'lambda_k2': jax.random.normal(ks[8], (D,), jnp.float32) * 0.1, 'ln_w': 1.0 + 0.1 * jax.random.normal(ks[9], (2 * D,), jnp.float32), 'ln_b': jnp.zeros((2 * D,), jnp.float32)}
    _L0_attn_in = _L0_attn_setup()

    def _L0_ffn_setup():
        import jax, jax.numpy as jnp
        import numpy as np
        N_EMBD = 256
        N_EXP = 8
        TOP_K = 2
        CAPACITY = 1024
        D_FF = 3 * N_EMBD
        key = jax.random.key(seed)
        k1, k2, k3, k4 = jax.random.split(key, 4)
        x = jax.random.normal(k1, (8, 512, N_EMBD), dtype=jnp.float32)
        w_gate = jax.random.normal(k2, (N_EMBD, N_EXP), dtype=jnp.float32) * 0.02
        c_fc = jax.random.normal(k3, (N_EXP, N_EMBD, D_FF), dtype=jnp.float32) * 0.02
        c_proj = jax.random.normal(k4, (N_EXP, D_FF // 2, N_EMBD), dtype=jnp.float32) * 0.02
        return {'x': x, 'w_gate': w_gate, 'c_fc': c_fc, 'c_proj': c_proj}
    _L0_ffn_in = _L0_ffn_setup()
    _d = {'L0_attn_x': _L0_attn_in['x'], 'L0_attn_Wq': _L0_attn_in['Wq'], 'L0_attn_Wk': _L0_attn_in['Wk'], 'L0_attn_Wv': _L0_attn_in['Wv'], 'L0_attn_Wo': _L0_attn_in['Wo'], 'L0_attn_lambda_q1': _L0_attn_in['lambda_q1'], 'L0_attn_lambda_k1': _L0_attn_in['lambda_k1'], 'L0_attn_lambda_q2': _L0_attn_in['lambda_q2'], 'L0_attn_lambda_k2': _L0_attn_in['lambda_k2'], 'L0_attn_ln_w': _L0_attn_in['ln_w'], 'L0_attn_ln_b': _L0_attn_in['ln_b'], 'L0_ffn_w_gate': _L0_ffn_in['w_gate'], 'L0_ffn_c_fc': _L0_ffn_in['c_fc'], 'L0_ffn_c_proj': _L0_ffn_in['c_proj']}
    _x0 = _d['L0_attn_x']
    _d['L0_attn_x'] = jax.random.normal(jax.random.fold_in(jax.random.key(seed), 1), (2, 4096, 256), dtype=_x0.dtype)
    del _x0
    return _d

def reference(L0_attn_x, L0_attn_Wq, L0_attn_Wk, L0_attn_Wv, L0_attn_Wo, L0_attn_lambda_q1, L0_attn_lambda_k1, L0_attn_lambda_q2, L0_attn_lambda_k2, L0_attn_ln_w, L0_attn_ln_b, L0_ffn_w_gate, L0_ffn_c_fc, L0_ffn_c_proj):

    def _L0_attn_ref(x, Wq, Wk, Wv, Wo, lambda_q1, lambda_k1, lambda_q2, lambda_k2, ln_w, ln_b):
        import jax, jax.numpy as jnp
        import numpy as np
        import math
        EMBED_DIM = 256
        NUM_HEADS = 8
        DEPTH = 12
        HEAD_DIM = EMBED_DIM // NUM_HEADS // 2
        LAMBDA_INIT = 0.8 - 0.6 * math.exp(-0.3 * DEPTH)
        EPS = 1e-08

        def _rotary(t):
            d = t.shape[-1]
            s = t.shape[1]
            inv_freq = 1.0 / 10000.0 ** (jnp.arange(0, d, 2, dtype=jnp.float32) / d)
            pos = jnp.arange(s, dtype=jnp.float32)
            freqs = pos[:, None] * inv_freq[None, :]
            freqs = jnp.repeat(freqs, 2, axis=-1)
            cos = jnp.cos(freqs)[None, :, None, :]
            sin = jnp.sin(freqs)[None, :, None, :]
            x = t.reshape(t.shape[:-1] + (d // 2, 2))
            x1, x2 = (x[..., 0], x[..., 1])
            rot = jnp.stack([-x2, x1], axis=-1).reshape(t.shape)
            return t * cos + rot * sin

        def _sdpa_over_heads(q, k, v):
            scores = jnp.einsum('bsnd,bsmd->bsnm', q, k) / HEAD_DIM ** 0.25
            aw = jax.nn.softmax(scores, axis=-1)
            return jnp.einsum('bsnm,bsme->bsne', aw, v)
        b, s, E = x.shape
        H, D = (NUM_HEADS, HEAD_DIM)
        q = (x @ Wq).reshape(b, s, 2 * H, D)
        k = (x @ Wk).reshape(b, s, 2 * H, D)
        v = (x @ Wv).reshape(b, s, H, 2 * D)
        q = _rotary(q)
        k = _rotary(k)
        q = q.reshape(b, s, H, 2, D)
        k = k.reshape(b, s, H, 2, D)
        q1, q2 = (q[:, :, :, 0], q[:, :, :, 1])
        k1, k2 = (k[:, :, :, 0], k[:, :, :, 1])
        attn1 = _sdpa_over_heads(q1, k1, v)
        attn2 = _sdpa_over_heads(q2, k2, v)
        lam = jnp.exp(jnp.sum(lambda_q1 * lambda_k1)) - jnp.exp(jnp.sum(lambda_q2 * lambda_k2)) + LAMBDA_INIT
        a = attn1 - lam * attn2
        rms = jax.lax.rsqrt(jnp.mean(a * a, axis=-1, keepdims=True) + EPS)
        a = a * rms * ln_w + ln_b
        a = a * (1.0 - LAMBDA_INIT)
        return a.reshape(b, s, E) @ Wo

    def _L0_ffn_ref(x, w_gate, c_fc, c_proj):
        import jax, jax.numpy as jnp
        import numpy as np
        N_EMBD = 256
        N_EXP = 8
        TOP_K = 2
        CAPACITY = 1024
        D_FF = 3 * N_EMBD
        B, T, d = x.shape
        N = B * T
        xf = x.reshape(N, d)
        scores = jax.nn.softmax(xf @ w_gate, axis=-1)
        weights, idx = jax.lax.top_k(scores, TOP_K)
        flat_e = idx.reshape(-1)
        tok = jnp.repeat(jnp.arange(N), TOP_K)
        oh = jax.nn.one_hot(flat_e, N_EXP, dtype=jnp.int32)
        pos = (jnp.cumsum(oh, axis=0) * oh).sum(-1) - 1
        valid = pos < CAPACITY
        pos_c = jnp.where(valid, pos, 0)
        vmask = valid.astype(x.dtype)[:, None]
        exp_x = jnp.zeros((N_EXP, CAPACITY, d), x.dtype)
        exp_x = exp_x.at[flat_e, pos_c].add(xf[tok] * vmask)
        h = jnp.einsum('ecd,edf->ecf', exp_x, c_fc)
        a, g = jnp.split(h, 2, axis=-1)
        h = jax.nn.silu(a) * g
        exp_out = jnp.einsum('ecf,efd->ecd', h, c_proj)
        gathered = exp_out[flat_e, pos_c]
        w = weights.reshape(-1)[:, None] * vmask
        out = (gathered * w).reshape(N, TOP_K, d).sum(axis=1)
        return out.reshape(B, T, d)
    x = L0_attn_x
    x = x + _L0_attn_ref(_layernorm(x, axis=-1), L0_attn_Wq, L0_attn_Wk, L0_attn_Wv, L0_attn_Wo, L0_attn_lambda_q1, L0_attn_lambda_k1, L0_attn_lambda_q2, L0_attn_lambda_k2, L0_attn_ln_w, L0_attn_ln_b)
    x = x + _L0_ffn_ref(_layernorm(x, axis=-1), L0_ffn_w_gate, L0_ffn_c_fc, L0_ffn_c_proj)
    return x

_drawn_inputs = setup_inputs


def setup_inputs(seed=0):
    import zlib

    import numpy as np

    out = dict(_drawn_inputs(seed))
    spreads = {'L0_attn_ln_b': (0.0, 0.401)}
    factors = {'L0_attn_lambda_q1': 8.0,
     'L0_attn_lambda_k1': 2.748,
     'L0_attn_lambda_q2': 8.0,
     'L0_attn_lambda_k2': 8.0,
     'L0_ffn_w_gate': 8.0,
     'L0_ffn_c_fc': 8.0,
     'L0_ffn_c_proj': 8.0}
    for name, (base, spread) in spreads.items():
        noise = np.random.default_rng([zlib.crc32(name.encode()), seed]).standard_normal(out[name].shape)
        drawn = base * np.exp(spread * noise) if base else spread * noise
        out[name] = jnp.asarray(drawn.astype(out[name].dtype))
    for name, factor in factors.items():
        out[name] = (out[name] * factor).astype(out[name].dtype)
    return out
```

```python
import math

import concourse.bass as bass
from concourse import mybir
from contextlib import ExitStack

P = 128
E = 256
H = 8
D = 16
DV = 2 * D
CAP = 1024
NEXP = 8
FF = 384
EPS_LN = 1e-5
EPS_RMS = 1e-8
LAMBDA_INIT = 0.8 - 0.6 * math.exp(-0.3 * 12)
SCORE_SCALE = 1.0 / D ** 0.25
COL_EXP, COL_W, COL_TOK, ROW = E, E + 2, E + 4, E + 8
OUT_OF_TABLE = float(1 << 20)
POOL_HEADS = 7

F32 = mybir.dt.float32
BF16 = mybir.dt.bfloat16
I32 = mybir.dt.int32
U32 = mybir.dt.uint32
ALU = mybir.AluOpType
ACT = mybir.ActivationFunctionType
AX_X = mybir.AxisListType.X


def build_block(nc, x, wq, wk, wv, wo, lq1, lk1, lq2, lk2, ln_w, ln_b, w_gate, c_fc, c_proj, out):
    NTOK = x.shape[0] * x.shape[1]
    NT = NTOK // P
    NBLK = CAP // P
    CB = 4
    NCH = NBLK // CB
    SLOTS = NEXP * CAP
    x_rows = x.rearrange("b s e -> (b s) e")
    table = nc.dram_tensor("slot_table", [SLOTS, ROW], F32, kind="Internal").ap()

    with ExitStack() as ctx:
        def sb(name, shape, dt=F32):
            return ctx.enter_context(nc.sbuf_tensor(name, shape, dt))

        def pb(name, shape, dt=F32):
            return ctx.enter_context(nc.psum_tensor(name, shape, dt))

        def sem(name):
            return ctx.enter_context(nc.semaphore(name))

        x_all = sb("x_all", [P, NT, E])
        wqkv = sb("wqkv", [P, 2, 3 * E])
        wo_sb = sb("wo_sb", [P, 2, E])
        wg_sb = sb("wg_sb", [P, 2, NEXP])
        ident = sb("ident", [P, P])
        tri = sb("tri", [P, P], BF16)
        ones = sb("ones", [P, P], BF16)
        ebase = sb("ebase", [1, NEXP], BF16)
        elimit = sb("elimit", [P, NEXP])
        eiota = sb("eiota", [P, NEXP])
        tok_all = sb("tok_all", [P, NT])
        lam_in = sb("lam_in", [P, 2, 2, D])
        lam_prod = sb("lam_prod", [P, 2, D])
        lam_sum = sb("lam_sum", [P, 2])
        lam_exp = sb("lam_exp", [P, 2])
        neg_lam = sb("neg_lam", [P, 1])
        lnwb = sb("lnwb", [P, 2])
        lnwb_s = sb("lnwb_s", [P, 2])
        fill = sb("fill", [P, NBLK, ROW])
        zeros = sb("zeros", [P, NBLK, E])
        two = range(2)
        st1 = [sb(f"st1{b}", [P, 6]) for b in two] * 2
        mv1 = [sb(f"mv1{b}", [P, 2]) for b in two] * 2
        ln_v1 = [sb(f"ln_v1{b}", [P, 1]) for b in two] * 2
        ln_v2 = [sb(f"ln_v2{b}", [P, 1]) for b in two] * 2
        ln_ms = [sb(f"ln_ms{b}", [P, H]) for b in two] * 2
        eps_ln = sb("eps_ln", [P, 1])
        eps_rms = sb("eps_rms", [P, 1])
        rs1 = [sb(f"rs1{b}", [P, 1]) for b in two] * 2
        xn = [sb(f"xn{b}", [P, E]) for b in two] * 2
        xT = [sb(f"xT{b}", [P, 2, P]) for b in two] * 2
        k_sb = [sb(f"k_sb{b}", [P, E]) for b in two] * 2
        v_sb = [sb(f"v_sb{b}", [P, E]) for b in two] * 2
        qk_prod = sb("qk_prod", [P, H * H * 2 * D])
        s_raw = [sb(f"s_raw{b}", [P, H, H, 2]) for b in two] * 2
        s_max = [sb(f"s_max{b}", [P, H, 2]) for b in two] * 2
        s_sub = [sb(f"s_sub{b}", [P, 2, H, H]) for b in two] * 2
        probs = [sb(f"probs{b}", [P, 2, H, H]) for b in two] * 2
        p_sum = [sb(f"p_sum{b}", [P, 2 * H]) for b in two] * 2
        p_rec = [sb(f"p_rec{b}", [P, 2 * H]) for b in two] * 2
        p_norm = [sb(f"p_norm{b}", [P, 2, H, H]) for b in two] * 2
        w_att = [sb(f"w_att{b}", [P, H, H]) for b in two] * 2
        v_prod = [sb(f"v_prod{b}", [P, H, H, DV]) for b in two] * 2
        a_sb = [sb(f"a_sb{b}", [P, E]) for b in two] * 2
        a_sq = [sb(f"a_sq{b}", [P, H, DV]) for b in two] * 2
        a_ms = [sb(f"a_ms{b}", [P, H]) for b in two] * 2
        a_rms = [sb(f"a_rms{b}", [P, H]) for b in two] * 2
        a_n = [sb(f"a_n{b}", [P, E]) for b in two] * 2
        aT = [sb(f"aT{b}", [P, 2, P]) for b in two] * 2
        st2 = [sb(f"st2{b}", [P, 6]) for b in two] * 2
        mv2 = [sb(f"mv2{b}", [P, 2]) for b in two] * 2
        rs2 = [sb(f"rs2{b}", [P, 1]) for b in two] * 2
        row = [sb(f"row{b}", [P, ROW]) for b in range(4)]
        x2T = [sb(f"x2T{b}", [P, 2, P]) for b in two] * 2
        g_nmax = [sb(f"g_nmax{b}", [P, 1]) for b in two] * 2
        g_exp = [sb(f"g_exp{b}", [P, NEXP]) for b in two] * 2
        g_sum = [sb(f"g_sum{b}", [P, 1]) for b in two] * 2
        g_rec = [sb(f"g_rec{b}", [P, 1]) for b in two] * 2
        g_top = [sb(f"g_top{b}", [P, 8]) for b in two] * 2
        g_idx = [sb(f"g_idx{b}", [P, 8], U32) for b in two] * 2
        g_hot = [sb(f"g_hot{b}", [P, 2, NEXP]) for b in two] * 2
        g_mask = [sb(f"g_mask{b}", [P, NEXP], BF16) for b in two] * 2
        g_before = [sb(f"g_before{b}", [P, NEXP], BF16) for b in two] * 2
        g_over = [sb(f"g_over{b}", [P, NEXP]) for b in two] * 2
        g_slot8 = [sb(f"g_slot8{b}", [P, NEXP]) for b in two] * 2
        g_sel = [sb(f"g_sel{b}", [P, 2, NEXP]) for b in two] * 2
        g_slotf = [sb(f"g_slotf{b}", [P, 2]) for b in two] * 2
        g_slot = [sb(f"g_slot{b}", [P, 2], I32) for b in range(4)]
        w1 = [sb(f"w1{b}", [P, 2, 2 * FF]) for b in two]
        w2 = [sb(f"w2{b}", [P, FF // P, E]) for b in two]
        xe = [sb(f"xe{b}", [P, CB, ROW]) for b in two]
        xeT = [sb(f"xeT{b}", [P, 2, CB * P]) for b in two]
        e_now = sb("e_now", [P, 1])
        e_hit = [sb(f"e_hit{b}", [P, CB, 2]) for b in two]
        e_w2 = [sb(f"e_w2{b}", [P, CB, 2]) for b in two]
        e_w = [sb(f"e_w{b}", [P, CB]) for b in two]
        e_tok = [sb(f"e_tok{b}", [P, CB], I32) for b in two]
        silu = [sb(f"silu{b}", [P, CB * P]) for b in two]
        hT = [sb(f"hT{b}", [P, FF // P, CB * P]) for b in two]
        y_sb = [sb(f"y_sb{b}", [P, CB, E]) for b in two]

        bank_t = pb("bank_t", [P, 4, P])
        bank_t2 = pb("bank_t2", [P, 4, P])
        bank_qk = [pb(f"bank_qk{b}", [P, 2, E]) for b in two] * 2
        bank_v = pb("bank_v", [P, 2, E])
        bank_a = pb("bank_a", [P, 2, E])
        bank_wo = pb("bank_wo", [P, 2, E])
        bank_g = pb("bank_g", [P, 2, E])
        logits, slots_ps = bank_g[:, 0, 0:NEXP], bank_g[:, 1, 0:NEXP]
        p2_xT = [bank_t, bank_t2]
        p2_h = [[bank_qk[0], bank_qk[1]], [bank_v, bank_a]]
        p2_y = [bank_wo, bank_g]

        x_loaded = [sem(f"x_loaded{c}") for c in range(4)]
        w_loaded = sem("w_loaded")
        consts = sem("consts")
        pool_chain = sem("pool_chain")
        lam_chain = sem("lam_chain")
        lam_ready = sem("lam_ready")
        filled = sem("filled")
        ln1_stats, ln1_aggr, ln1_rstd, xn_ready = sem("ln1_stats"), sem("ln1_aggr"), sem("ln1_rstd"), sem("xn_ready")
        a_copied = sem("a_copied")
        ln1_log, ln2_log = sem("ln1_log"), sem("ln2_log")
        xn_transposed, xT_copied, qkv_done = sem("xn_transposed"), sem("xT_copied"), sem("qkv_done")
        k_copied, v_copied, qk_multiplied = sem("k_copied"), sem("v_copied"), sem("qk_multiplied")
        scores_ready, smax_ready, ssub_ready, exp_done = sem("scores_ready"), sem("smax_ready"), sem("ssub_ready"), sem("exp_done")
        psum_ready, prec_ready, pnorm_ready, w_ready = sem("psum_ready"), sem("prec_ready"), sem("pnorm_ready"), sem("w_ready")
        pv_vector, pv_pool, a_summed = sem("pv_vector"), sem("pv_pool"), sem("a_summed")
        sq_done, ms_ready, ms_log, rms_ready, an_ready = sem("sq_done"), sem("ms_ready"), sem("ms_log"), sem("rms_ready"), sem("an_ready")
        an_transposed, aT_copied, wo_done, x1_ready = sem("an_transposed"), sem("aT_copied"), sem("wo_done"), sem("x1_ready")
        ln2_stats, ln2_aggr, ln2_rstd, xn2_ready = sem("ln2_stats"), sem("ln2_aggr"), sem("ln2_rstd"), sem("xn2_ready")
        xn2_transposed, x2T_copied, logits_ready = sem("xn2_transposed"), sem("x2T_copied"), sem("logits_ready")
        gmax_ready, gexp_done, gtop_ready, gidx_ready = sem("gmax_ready"), sem("gexp_done"), sem("gtop_ready"), sem("gidx_ready")
        grec_ready, gexperts_ready, ghot_ready, gmask_ready = sem("grec_ready"), sem("gexperts_ready"), sem("ghot_ready"), sem("gmask_ready")
        before_ready, row_ready, pos_ready = sem("before_ready"), sem("row_ready"), sem("pos_ready")
        over_ready, slot8_ready, sel_ready, slotf_ready, slot_ready = sem("over_ready"), sem("slot8_ready"), sem("sel_ready"), sem("slotf_ready"), sem("slot_ready")
        tok_written = sem("tok_written")
        scattered = [sem(f"scattered{r}") for r in range(4)]
        x1_stored = sem("x1_stored")
        e_loaded = [sem(f"e_loaded{b}") for b in two]
        xe_loaded = [sem(f"xe_loaded{b}") for b in two]
        e_number = sem("e_number")
        hit_ready, wsel_ready, wts_ready, toks_ready = sem("hit_ready"), sem("wsel_ready"), sem("wts_ready"), sem("toks_ready")
        xe_transposed = sem("xe_transposed")
        xeT_scalar, xeT_vector = sem("xeT_scalar"), sem("xeT_vector")
        h_done = sem("h_done")
        silu_done, h_ready = sem("silu_done"), sem("h_ready")
        y_done = sem("y_done")
        y_scaled = sem("y_scaled")
        y_added = [sem(f"y_added{b}") for b in two]

        def past(eng, s, t, back=0, per=1):
            if isinstance(t, int):
                if t - back < 0:
                    return
            eng.wait_ge(s, (t - (back - 1)) * per)

        UNROLL = 4
        LAG_MAX = 9
        FIRST = LAG_MAX + 3

        def row_free(eng, t, r):
            if isinstance(t, int) and t < UNROLL:
                return
            eng.wait_ge(scattered[r], (t - r) * (32 // UNROLL))

        def run_tiles(eng, step):
            for i in range(FIRST):
                step(i, i % UNROLL)
            with eng.Fori(0, (NT - FIRST) // UNROLL) as turn:
                for u in range(UNROLL):
                    step(turn * UNROLL + (FIRST + u), u)
            for i in range(NT, NT + LAG_MAX):
                step(i, i % UNROLL)

        def live(i, lag):
            return not isinstance(i, int) or 0 <= i - lag < NT

        def x_tile(t):
            if isinstance(t, int):
                return x_all[:, t, :]
            return x_all[:, bass.ds(t, 1), :].rearrange("p a e -> p (a e)")

        block = ctx.enter_context(nc.Block())

        @block.sync
        def _(sp):
            xv = x_rows.rearrange("(t p) e -> p t e", p=P)
            parts = [(0, 2), (2, 8), (8, 32), (32, NT)]
            sp.dma_start(x_all[:, 0:2, :], xv[:, 0:2, :]).then_inc(x_loaded[0], 16)
            for j, w in enumerate((wq, wk, wv)):
                sp.dma_start(wqkv[:, :, j * E:(j + 1) * E], w.rearrange("(k p) n -> p k n", p=P)).then_inc(w_loaded, 16)
            for c in range(1, 4):
                a, b = parts[c]
                sp.dma_start(x_all[:, a:b, :], xv[:, a:b, :]).then_inc(x_loaded[c], 16)
            sp.wait_ge(consts, 1)
            for e in range(NEXP):
                sp.dma_start(table[e * CAP:(e + 1) * CAP, :].rearrange("(b p) w -> p b w", p=P), fill[:, :, :]).then_inc(filled, 16)
            sp.dma_start(out[NTOK:NTOK + CAP, :].rearrange("(b p) w -> p b w", p=P), zeros[:, :, :]).then_inc(filled, 16)
            for e in range(2):
                sp.dma_start(w1[e][:, :, :], c_fc[e].rearrange("(k p) f -> p k f", p=P)).then_inc(e_loaded[e], 16)
                sp.dma_start(w2[e][:, :, :], c_proj[e].rearrange("(k p) n -> p k n", p=P)).then_inc(e_loaded[e], 16)
            ov = out[0:NTOK, :].rearrange("(t p) e -> p t e", p=P)
            for c in range(NT // 8):
                sp.wait_ge(x1_ready, 8 * (c + 1))
                sp.dma_start(ov[:, 8 * c:8 * c + 8, :], x_all[:, 8 * c:8 * c + 8, :]).then_inc(x1_stored, 16)
            for r in range(UNROLL):
                sp.wait_ge(scattered[r], 32 * NT // UNROLL)
            sp.wait_ge(filled, 16 * (NEXP + 1))

            def load_chunk(e, c, b):
                n = e * NCH + c
                past(sp, xe_transposed, n, 2, 2)
                past(sp, hit_ready, n, 2)
                past(sp, wsel_ready, n, 2)
                past(sp, toks_ready, n, 2)
                src = table.rearrange("(n b p) w -> n p b w", b=CB, p=P)
                s = src[n] if isinstance(n, int) else src[bass.ds(n, 1)].rearrange("n p b w -> (n p) b w")
                sp.dma_start(xe[b][:, :, :], s).then_inc(xe_loaded[b], 16)

            def load_expert(e, b):
                past(sp, y_done, e, 2, 2 * NCH)
                c1, c2 = c_fc, c_proj
                s1 = c1[bass.ds(e, 1)].rearrange("a (k p) f -> p (a k) f", p=P)
                s2 = c2[bass.ds(e, 1)].rearrange("a (k p) f -> p (a k) f", p=P)
                sp.dma_start(w1[b][:, :, :], s1).then_inc(e_loaded[b], 16)
                sp.dma_start(w2[b][:, :, :], s2).then_inc(e_loaded[b], 16)

            for e in range(2):
                for c in range(NCH):
                    load_chunk(e, c, c % 2)
            with sp.Fori(1, NEXP // 2) as h:
                for u in range(2):
                    load_expert(h * 2 + u, u)
                    for c in range(NCH):
                        load_chunk(h * 2 + u, c, c % 2)

        @block.gpsimd
        def _(pool):
            n = 0

            def chain(ins):
                nonlocal n
                ins.then_inc(pool_chain, 1)
                n += 1

            chain(pool.memset(ident[:, :], 0.0))
            pool.wait_ge(pool_chain, n)
            chain(pool.affine_select(out=ident[:, :], in_=ident[:, :], compare_op=ALU.not_equal, fill=1.0, base=0,
                                     pattern=[[-1, P]], channel_multiplier=1))
            chain(pool.memset(fill[:, :, :], 0.0))
            chain(pool.memset(zeros[:, :, :], 0.0))
            chain(pool.memset(ones[:, :], 1.0))
            chain(pool.memset(eps_ln[:, :], EPS_LN))
            chain(pool.memset(eps_rms[:, :], EPS_RMS * DV))
            pool.wait_ge(pool_chain, n)
            chain(pool.iota(fill[:, :, COL_TOK], pattern=[[P, NBLK]], base=NTOK, channel_multiplier=1,
                            allow_small_or_imprecise_dtypes=True))
            pool.wait_ge(pool_chain, n)
            pool.nop().then_inc(consts, 1)
            for i, (t, step, base) in enumerate(((eiota, 1, 0), (elimit, CAP, CAP))):
                chain(pool.iota(t[:, :], pattern=[[step, NEXP]], base=base, channel_multiplier=0,
                                allow_small_or_imprecise_dtypes=True))
            chain(pool.iota(ebase[:, :], pattern=[[CAP, NEXP]], base=0, channel_multiplier=0,
                            allow_small_or_imprecise_dtypes=True))
            chain(pool.iota(tok_all[:, :], pattern=[[P, NT]], base=0, channel_multiplier=1,
                            allow_small_or_imprecise_dtypes=True))
            chain(pool.affine_select(out=tri[:, :], in_=ones[:, :], compare_op=ALU.is_gt, fill=0.0, base=0,
                                     pattern=[[1, P]], channel_multiplier=-1))
            for r in row:
                chain(pool.memset(r[:, :], 0.0))
            chain(pool.memset(g_before[0][:, :], 0.0))
            pool.wait_ge(pool_chain, n)
            pool.nop().then_inc(consts, 1)

            def products(t, b):
                past(pool, w_ready, t)
                past(pool, v_copied, t)
                past(pool, a_summed, t, 2)
                nh = POOL_HEADS
                pool.tensor_tensor(
                    v_prod[b][:, :, 0:nh, :],
                    w_att[b][:, 0:nh, :].rearrange("p n m -> p m n").unsqueeze(3).to_broadcast([P, H, nh, DV]),
                    v_sb[b][:, :].rearrange("p (m e) -> p m e", m=H).unsqueeze(2).to_broadcast([P, H, nh, DV]),
                    ALU.mult).then_inc(pv_pool, 1)

            def token_numbers(t, b):
                row_free(pool, t, b)
                src = tok_all[:, t:t + 1] if isinstance(t, int) else tok_all[:, bass.ds(t, 1)]
                pool.tensor_copy(row[b][:, COL_TOK:COL_TOK + 1], src).then_inc(tok_written, 1)

            def row_waits(t):
                past(pool, slot_ready, t)
                past(pool, row_ready, t)
                past(pool, gexperts_ready, t)
                past(pool, xn2_ready, t)
                past(pool, tok_written, t)
                if isinstance(t, int) and t == 0:
                    pool.wait_ge(filled, 16 * (NEXP + 1))

            def scatter(t, b):
                for k in range(2):
                    pool.indirect_dma_start(
                        out=table, out_offset=bass.IndirectOffsetOnAxis(ap=g_slot[b][:, k:k + 1], axis=0),
                        in_=row[b][:, :], in_offset=None, bounds_check=SLOTS - 1, oob_is_err=False,
                    ).then_inc(scattered[b], 16)

            def step(i, u):
                if live(i, 9):
                    row_waits(i - 9)
                if live(i, 3):
                    products(i - 3, (u - 3) % UNROLL)
                if live(i, 9):
                    scatter(i - 9, (u - 9) % UNROLL)
                if live(i, 8):
                    token_numbers(i - 8, (u - 8) % UNROLL)

            run_tiles(pool, step)

            pool.wait_ge(x1_stored, 16 * (NT // 8))

            def add_chunk(e, c):
                n = e * NCH + c
                past(pool, toks_ready, n)
                if c == 0:
                    for b in two:
                        pool.wait_ge(y_added[b], 16 * CB * (NCH // 2) * e)
                for k in range(CB):
                    pool.wait_ge(y_scaled, n * CB + k + 1)
                    pool.indirect_dma_start(
                        out=out, out_offset=bass.IndirectOffsetOnAxis(ap=e_tok[c % 2][:, k:k + 1], axis=0),
                        in_=y_sb[c % 2][:, k, :], in_offset=None, compute_op=ALU.add,
                    ).then_inc(y_added[c % 2], 16)

            for e in range(NEXP):
                for c in range(NCH):
                    add_chunk(e, c)
            for b in two:
                pool.wait_ge(y_added[b], 16 * CB * (NCH // 2) * NEXP)

        @block.scalar
        def _(act):
            act.dma_start(lam_in[:, 0, 0, :], lq1.rearrange("(a d) -> a d", a=1).to_broadcast([P, D])).then_inc(w_loaded, 16)
            act.dma_start(lam_in[:, 0, 1, :], lk1.rearrange("(a d) -> a d", a=1).to_broadcast([P, D])).then_inc(w_loaded, 16)
            act.dma_start(lam_in[:, 1, 0, :], lq2.rearrange("(a d) -> a d", a=1).to_broadcast([P, D])).then_inc(w_loaded, 16)
            act.dma_start(lam_in[:, 1, 1, :], lk2.rearrange("(a d) -> a d", a=1).to_broadcast([P, D])).then_inc(w_loaded, 16)
            for r in range(P // DV):
                act.dma_start(lnwb[r * DV:(r + 1) * DV, 0:1], ln_w.rearrange("(d a) -> d a", a=1)).then_inc(w_loaded, 16)
                act.dma_start(lnwb[r * DV:(r + 1) * DV, 1:2], ln_b.rearrange("(d a) -> d a", a=1)).then_inc(w_loaded, 16)
            act.dma_start(wo_sb[:, :, :], wo.rearrange("(k p) n -> p k n", p=P)).then_inc(w_loaded, 16)
            act.dma_start(wg_sb[:, :, :], w_gate.rearrange("(k p) n -> p k n", p=P)).then_inc(w_loaded, 16)
            act.wait_ge(lam_chain, 2)
            act.wait_ge(consts, 2)
            nc.scalar.activation(lam_exp[:, :], lam_sum[:, :], ACT.Exp).then_inc(lam_ready, 1)

            def copy_xT(t, b):
                past(act, xn_transposed, t)
                past(act, qkv_done, t, 2)
                nc.scalar.copy(xT[b][:, :, :], bank_t[:, 0:2, :]).then_inc(xT_copied, 1)

            def copy_kv(t, b):
                past(act, qkv_done, t)
                past(act, qk_multiplied, t, 2)
                nc.scalar.copy(k_sb[b][:, :], bank_qk[b][:, 1, :]).then_inc(k_copied, 1)
                past(act, pv_pool, t, 2)
                past(act, pv_vector, t, 2)
                nc.scalar.copy(v_sb[b][:, :], bank_v[:, 0, :]).then_inc(v_copied, 1)

            def exp_scores(t, b):
                past(act, ssub_ready, t)
                past(act, pnorm_ready, t, 2)
                nc.scalar.activation(probs[b][:, :, :, :], s_sub[b][:, :, :, :], ACT.Exp, scale=SCORE_SCALE).then_inc(exp_done, 1)

            def square(t, b):
                past(act, a_summed, t)
                past(act, an_ready, t, 2)
                nc.scalar.copy(a_sb[b][:, :], bank_a[:, 0, :]).then_inc(a_copied, 1)
                past(act, a_copied, t)
                nc.scalar.activation(a_sq[b][:, :, :].rearrange("p n e -> p (n e)"), a_sb[b][:, :], ACT.Square).then_inc(sq_done, 1)

            def copy_aT(t, b):
                if isinstance(t, int) and t == 0:
                    act.wait_ge(lam_ready, 3)
                past(act, an_transposed, t)
                past(act, wo_done, t, 2)
                nc.scalar.activation(aT[b][:, :, :], bank_t2[:, 2:4, :], ACT.Identity, bias=lnwb_s[:, 1:2],
                                     scale=lnwb_s[:, 0:1]).then_inc(aT_copied, 1)

            def copy_x2T(t, b):
                past(act, xn2_transposed, t)
                past(act, logits_ready, t, 2)
                nc.scalar.copy(x2T[b][:, :, :], bank_t2[:, 0:2, :]).then_inc(x2T_copied, 1)

            def exp_gate(t, b):
                past(act, gmax_ready, t)
                past(act, gidx_ready, t, 2)
                past(act, grec_ready, t, 2)
                nc.scalar.activation(g_exp[b][:, :], logits, ACT.Exp, bias=g_nmax[b][:, :],
                                     accum_out=g_sum[b][:, :]).then_inc(gexp_done, 1)

            def rstd1(t, b):
                past(act, ln1_aggr, t)
                nc.scalar.activation(ln_v1[b][:, :], mv1[b][:, 1:2], ACT.Ln, bias=eps_ln[:, :]).then_inc(ln1_log, 1)
                past(act, ln1_log, t)
                past(act, xn_ready, t, 2)
                nc.scalar.activation(rs1[b][:, :], ln_v1[b][:, :], ACT.Exp, scale=-0.5).then_inc(ln1_rstd, 1)

            def rstd2(t, b):
                past(act, ln2_aggr, t)
                nc.scalar.activation(ln_v2[b][:, :], mv2[b][:, 1:2], ACT.Ln, bias=eps_ln[:, :]).then_inc(ln2_log, 1)
                past(act, ln2_log, t)
                past(act, xn2_ready, t, 2)
                nc.scalar.activation(rs2[b][:, :], ln_v2[b][:, :], ACT.Exp, scale=-0.5).then_inc(ln2_rstd, 1)

            def rms_root(t, b):
                past(act, ms_ready, t)
                nc.scalar.activation(ln_ms[b][:, :], a_ms[b][:, :], ACT.Ln, bias=eps_rms[:, :]).then_inc(ms_log, 1)
                past(act, ms_log, t)
                past(act, an_ready, t, 2)
                nc.scalar.activation(a_rms[b][:, :], ln_ms[b][:, :], ACT.Exp, scale=-0.5).then_inc(rms_ready, 1)

            def step(i, u):
                if live(i, 5):
                    rms_root(i - 5, (u - 5) % UNROLL)
                if live(i, 2):
                    copy_kv(i - 2, (u - 2) % UNROLL)
                if live(i, 7):
                    copy_x2T(i - 7, (u - 7) % UNROLL)
                if live(i, 3):
                    exp_scores(i - 3, (u - 3) % UNROLL)
                if live(i, 4):
                    square(i - 4, (u - 4) % UNROLL)
                if live(i, 5):
                    copy_aT(i - 5, (u - 5) % UNROLL)
                if live(i, 1):
                    copy_xT(i - 1, (u - 1) % UNROLL)
                if live(i, 8):
                    exp_gate(i - 8, (u - 8) % UNROLL)
                if live(i, 6):
                    rstd2(i - 6, (u - 6) % UNROLL)
                if live(i, 0):
                    rstd1(i, u)

            run_tiles(act, step)

            def chunk(e, c):
                n, b = e * NCH + c, c % 2
                act.wait_ge(xe_transposed, n * 2 + 1)
                past(act, h_done, n, 2, 3)
                nc.scalar.copy(xeT[b][:, 0, :], p2_xT[0][:, :, :].rearrange("p b q -> p (b q)")).then_inc(xeT_scalar, 1)
                for j in range(FF // P):
                    act.wait_ge(h_done, n * 3 + j + 1)
                    m = n * 3 + j
                    past(act, h_ready, m, 2)
                    q = (c * 3 + j) % 2
                    nc.scalar.activation(silu[q][:, :], p2_h[q][0][:, :, :].rearrange("p b q -> p (b q)"),
                                         ACT.Silu).then_inc(silu_done, 1)
                act.wait_ge(wts_ready, n + 1)
                for k in range(CB):
                    act.wait_ge(y_done, n * 2 + k // 2 + 1)
                    if k == 0:
                        past(act, y_added[b], e * (NCH // 2) + c // 2, 1, 16 * CB)
                    nc.scalar.activation(y_sb[b][:, k, :], p2_y[k // 2][:, k % 2, :], ACT.Copy, scale=e_w[b][:, k:k + 1]).then_inc(y_scaled, 1)

            for c in range(NCH):
                chunk(0, c)
            with act.Fori(1, NEXP) as e:
                for c in range(NCH):
                    chunk(e, c)

        @block.tensor
        def _(pe):
            pe.wait_ge(w_loaded, 16 * (3 + 4 + 2 * (P // DV) + 2))
            pe.wait_ge(consts, 2)

            def transpose_x(t, b):
                past(pe, xn_ready, t)
                past(pe, xT_copied, t, 1)
                for k in range(2):
                    last = nc.tensor.transpose(bank_t[:, k, :], xn[b][:, k * P:(k + 1) * P], ident[:, :])
                last.then_inc(xn_transposed, 1)

            def project(t, b):
                past(pe, xT_copied, t)
                past(pe, qk_multiplied, t, 2)
                for k in range(2):
                    nc.tensor.matmul(bank_qk[b][:, :, :].rearrange("p a e -> p (a e)"), xT[b][:, k, :],
                                     wqkv[:, k, 0:2 * E], start=(k == 0), stop=(k == 1))
                past(pe, v_copied, t, 1)
                for k in range(2):
                    last = nc.tensor.matmul(bank_v[:, 0, :], xT[b][:, k, :], wqkv[:, k, 2 * E:3 * E],
                                            start=(k == 0), stop=(k == 1))
                last.then_inc(qkv_done, 1)

            def sum_heads(t, b):
                past(pe, pv_vector, t)
                past(pe, pv_pool, t)
                past(pe, a_copied, t, 1)
                for m in range(H):
                    last = nc.tensor.matmul(bank_a[:, 0, :], ident[:, :],
                                            v_prod[b][:, m, :, :].rearrange("p n e -> p (n e)"),
                                            start=(m == 0), stop=(m == H - 1))
                last.then_inc(a_summed, 1)

            def transpose_a(t, b):
                past(pe, an_ready, t)
                past(pe, x2T_copied, t, 2)
                for k in range(2):
                    last = nc.tensor.transpose(bank_t2[:, 2 + k, :], a_n[b][:, k * P:(k + 1) * P], ident[:, :])
                last.then_inc(an_transposed, 1)

            def out_project(t, b):
                past(pe, aT_copied, t)
                past(pe, x1_ready, t, 1)
                for k in range(2):
                    last = nc.tensor.matmul(bank_wo[:, 0, :], aT[b][:, k, :], wo_sb[:, k, :], start=(k == 0), stop=(k == 1))
                last.then_inc(wo_done, 1)

            def transpose_x2(t, b):
                past(pe, xn2_ready, t)
                if isinstance(t, int):
                    pe.wait_ge(aT_copied, min(t + 2, NT))
                else:
                    pe.wait_ge(aT_copied, t + 2)
                for k in range(2):
                    last = nc.tensor.transpose(bank_t2[:, k, :], row[b][:, k * P:(k + 1) * P], ident[:, :])
                last.then_inc(xn2_transposed, 1)

            def gate(t, b):
                past(pe, x2T_copied, t)
                past(pe, slot8_ready, t, 1)
                for k in range(2):
                    last = nc.tensor.matmul(logits, x2T[b][:, k, :], wg_sb[:, k, :], start=(k == 0), stop=(k == 1))
                last.then_inc(logits_ready, 1)

            def positions(t, b):
                past(pe, gmask_ready, t)
                past(pe, gexp_done, t)
                if not (isinstance(t, int) and t == 0):
                    past(pe, before_ready, t, 1)
                nc.tensor.matmul(slots_ps, tri[:, :], g_mask[b][:, :], start=True, stop=False)
                nc.tensor.matmul(slots_ps, ones[:, :], g_before[b][:, :], start=False, stop=False)
                nc.tensor.matmul(slots_ps, ones[0:1, :], ebase[:, :], start=False, stop=True).then_inc(pos_ready, 1)

            def step(i, u):
                if live(i, 9):
                    positions(i - 9, (u - 9) % UNROLL)
                if live(i, 2):
                    project(i - 2, (u - 2) % UNROLL)
                if live(i, 6):
                    out_project(i - 6, (u - 6) % UNROLL)
                if live(i, 7):
                    transpose_x2(i - 7, (u - 7) % UNROLL)
                if live(i, 4):
                    sum_heads(i - 4, (u - 4) % UNROLL)
                if live(i, 8):
                    gate(i - 8, (u - 8) % UNROLL)
                if live(i, 5):
                    transpose_a(i - 5, (u - 5) % UNROLL)
                if live(i, 1):
                    transpose_x(i - 1, (u - 1) % UNROLL)

            run_tiles(pe, step)

            pe.wait_ge(slot8_ready, NT)
            pe.wait_ge(x2T_copied, NT)

            def chunk(e, c, wb):
                n, b = e * NCH + c, c % 2
                pe.wait_ge(xe_loaded[b], (n // 2 + 1) * 16 if isinstance(n, int) else (e * (NCH // 2) + c // 2 + 1) * 16)
                for k in range(2):
                    past(pe, (xeT_scalar, xeT_vector)[k], n, 1)
                    for q in range(CB):
                        last = nc.tensor.transpose(p2_xT[k][:, q, :], xe[b][:, q, k * P:(k + 1) * P], ident[:, :])
                    last.then_inc(xe_transposed, 1)
                pe.wait_ge(xeT_scalar, n + 1)
                pe.wait_ge(xeT_vector, n + 1)
                for j in range(FF // P):
                    m = n * 3 + j
                    past(pe, h_ready, m, 2)
                    q = (c * 3 + j) % 2
                    for half in range(2):
                        for k in range(2):
                            last = nc.tensor.matmul(
                                p2_h[q][half][:, :, :].rearrange("p b q -> p (b q)"),
                                w1[wb][:, k, half * FF + j * P:half * FF + (j + 1) * P], xeT[b][:, k, :],
                                start=(k == 0), stop=(k == 1))
                    last.then_inc(h_done, 1)
                pe.wait_ge(h_ready, n * 3 + 3)
                for k in range(CB):
                    if k % 2 == 0:
                        past(pe, y_scaled, n * CB + k + 1, CB)
                    for j in range(FF // P):
                        last = nc.tensor.matmul(p2_y[k // 2][:, k % 2, :], hT[b][:, j, k * P:(k + 1) * P], w2[wb][:, j, :],
                                                start=(j == 0), stop=(j == FF // P - 1))
                    if k % 2 == 1:
                        last.then_inc(y_done, 1)

            def expert(e, wb):
                pe.wait_ge(e_loaded[wb], (e // 2 + 1) * 32 if isinstance(e, int) else (e - wb) * 16 + 32)
                for c in range(NCH):
                    chunk(e, c, wb)

            for e in range(2):
                expert(e, e)
            with pe.Fori(1, NEXP // 2) as h:
                for u in range(2):
                    expert(h * 2 + u, u)

        @block.vector
        def _(dve):
            dve.wait_ge(w_loaded, 16 * (3 + 4 + 2 * (P // DV) + 2))
            nc.vector.tensor_tensor(lam_prod[:, :, :], lam_in[:, :, 0, :], lam_in[:, :, 1, :], ALU.mult).then_inc(lam_chain, 1)
            dve.wait_ge(lam_chain, 1)
            nc.vector.tensor_reduce(lam_sum[:, :], lam_prod[:, :, :], AX_X, ALU.add).then_inc(lam_chain, 1)
            nc.vector.tensor_scalar(lnwb_s[:, 0:1], lnwb[:, 0:1], (1.0 - LAMBDA_INIT) * math.sqrt(DV), None, ALU.mult).then_inc(lam_ready, 1)
            nc.vector.tensor_scalar(lnwb_s[:, 1:2], lnwb[:, 1:2], 1.0 - LAMBDA_INIT, None, ALU.mult).then_inc(lam_ready, 1)
            dve.wait_ge(lam_ready, 3)
            nc.vector.tensor_tensor(neg_lam[:, :], lam_exp[:, 1:2], lam_exp[:, 0:1], ALU.subtract).then_inc(lam_chain, 1)
            dve.wait_ge(lam_chain, 3)
            nc.vector.tensor_scalar(neg_lam[:, :], neg_lam[:, :], LAMBDA_INIT, None, ALU.subtract).then_inc(lam_chain, 1)
            nc.vector.memset(e_now[:, :], 0.0).then_inc(e_number, 1)
            dve.wait_ge(lam_chain, 4)
            dve.wait_ge(consts, 2)
            arrive = {0: 0, 2: 1, 8: 2, 32: 3}

            def stats1(t, b):
                if isinstance(t, int) and t in arrive:
                    dve.wait_ge(x_loaded[arrive[t]], 16)
                nc.vector.bn_stats(st1[b][:, :], x_tile(t)).then_inc(ln1_stats, 1)

            def aggregate1(t, b):
                nc.vector.bn_aggr(mv1[b][:, :], st1[b][:, :]).then_inc(ln1_aggr, 1)

            def normalise1(t, b):
                past(dve, ln1_rstd, t)
                past(dve, xn_transposed, t, 2)
                nc.vector.tensor_scalar(xn[b][:, :], x_tile(t), mv1[b][:, 0:1], rs1[b][:, :], ALU.subtract, ALU.mult).then_inc(xn_ready, 1)

            def scores(t, b):
                past(dve, k_copied, t)
                past(dve, scores_ready, t, 1)
                q4 = bank_qk[b][:, 0, :].rearrange("p (n f) -> p n f", n=H).unsqueeze(2).to_broadcast([P, H, H, DV])
                k4 = k_sb[b][:, :].rearrange("p (m f) -> p m f", m=H).unsqueeze(1).to_broadcast([P, H, H, DV])
                nc.vector.tensor_tensor(qk_prod[:, :].rearrange("p (n m f) -> p n m f", n=H, m=H), q4, k4, ALU.mult).then_inc(qk_multiplied, 1)
                past(dve, qk_multiplied, t)
                nc.vector.tensor_reduce(s_raw[b][:, :, :, :].rearrange("p n m c -> p (n m c)"),
                                        qk_prod[:, :].rearrange("p (s d) -> p s d", d=D), AX_X, ALU.add).then_inc(scores_ready, 1)
                past(dve, scores_ready, t)
                nc.vector.tensor_reduce(s_max[b][:, :, :], s_raw[b][:, :, :, :].rearrange("p n m c -> p n c m"),
                                        AX_X, ALU.max).then_inc(smax_ready, 1)
                past(dve, smax_ready, t)
                past(dve, exp_done, t, 2)
                nc.vector.tensor_tensor(s_sub[b][:, :, :, :].rearrange("p c n m -> p n m c"), s_raw[b][:, :, :, :],
                                        s_max[b][:, :, :].unsqueeze(2).to_broadcast([P, H, H, 2]), ALU.subtract).then_inc(ssub_ready, 1)

            def softmax(t, b):
                past(dve, exp_done, t)
                nc.vector.tensor_reduce(p_sum[b][:, :], probs[b][:, :, :, :].rearrange("p c n m -> p (c n) m"),
                                        AX_X, ALU.add).then_inc(psum_ready, 1)
                past(dve, psum_ready, t)
                nc.vector.reciprocal(p_rec[b][:, :], p_sum[b][:, :]).then_inc(prec_ready, 1)
                past(dve, prec_ready, t)
                nc.vector.tensor_tensor(p_norm[b][:, :, :, :].rearrange("p c n m -> p (c n) m"),
                                        probs[b][:, :, :, :].rearrange("p c n m -> p (c n) m"),
                                        p_rec[b][:, :].unsqueeze(2).to_broadcast([P, 2 * H, H]), ALU.mult).then_inc(pnorm_ready, 1)
                past(dve, pnorm_ready, t)
                past(dve, pv_pool, t, 2)
                nc.vector.scalar_tensor_tensor(out=w_att[b][:, :, :].rearrange("p n m -> p (n m)"),
                                               in0=p_norm[b][:, 1, :, :].rearrange("p n m -> p (n m)"), scalar=neg_lam[:, :],
                                               in1=p_norm[b][:, 0, :, :].rearrange("p n m -> p (n m)"),
                                               op0=ALU.mult, op1=ALU.add).then_inc(w_ready, 1)
                past(dve, w_ready, t)
                past(dve, v_copied, t)
                past(dve, a_summed, t, 2)
                n0, nh = POOL_HEADS, H - POOL_HEADS
                nc.vector.tensor_tensor(
                    v_prod[b][:, :, n0:H, :],
                    w_att[b][:, n0:H, :].rearrange("p n m -> p m n").unsqueeze(3).to_broadcast([P, H, nh, DV]),
                    v_sb[b][:, :].rearrange("p (m e) -> p m e", m=H).unsqueeze(2).to_broadcast([P, H, nh, DV]),
                    ALU.mult).then_inc(pv_vector, 1)

            def rms_sums(t, b):
                past(dve, sq_done, t)
                nc.vector.tensor_reduce(a_ms[b][:, :], a_sq[b][:, :, :], AX_X, ALU.add).then_inc(ms_ready, 1)

            def rms_scale(t, b):
                past(dve, rms_ready, t)
                past(dve, an_transposed, t, 2)
                nc.vector.tensor_tensor(a_n[b][:, :].rearrange("p (n e) -> p n e", n=H),
                                        a_sb[b][:, :].rearrange("p (n e) -> p n e", n=H),
                                        a_rms[b][:, :].unsqueeze(2).to_broadcast([P, H, DV]), ALU.mult).then_inc(an_ready, 1)

            def add_attention(t, b):
                past(dve, wo_done, t)
                nc.vector.tensor_tensor(x_tile(t), bank_wo[:, 0, :], x_tile(t), ALU.add).then_inc(x1_ready, 1)

            def stats2(t, b):
                nc.vector.bn_stats(st2[b][:, :], x_tile(t)).then_inc(ln2_stats, 1)

            def aggregate2(t, b):
                nc.vector.bn_aggr(mv2[b][:, :], st2[b][:, :]).then_inc(ln2_aggr, 1)

            def normalise2(t, b):
                past(dve, ln2_rstd, t)
                row_free(dve, t, b)
                nc.vector.tensor_scalar(row[b][:, 0:E], x_tile(t), mv2[b][:, 0:1], rs2[b][:, :], ALU.subtract, ALU.mult).then_inc(xn2_ready, 1)

            def gate_max(t, b):
                past(dve, logits_ready, t)
                nc.vector.tensor_reduce(g_nmax[b][:, :], logits, AX_X, ALU.max, negate=True).then_inc(gmax_ready, 1)

            def gate_reciprocal(t, b):
                past(dve, gexp_done, t)
                nc.vector.reciprocal(g_rec[b][:, :], g_sum[b][:, :]).then_inc(grec_ready, 1)

            def route(t, b):
                nc.vector.max(g_top[b][:, :], g_exp[b][:, :]).then_inc(gtop_ready, 1)
                past(dve, grec_ready, t)
                past(dve, gtop_ready, t)
                nc.vector.tensor_scalar(row[b][:, COL_W:COL_W + 2], g_top[b][:, 0:2], g_rec[b][:, :], None, ALU.mult).then_inc(row_ready, 1)
                nc.vector.max_index(g_idx[b][:, :], g_top[b][:, :], g_exp[b][:, :]).then_inc(gidx_ready, 1)
                past(dve, gidx_ready, t)
                nc.vector.tensor_copy(row[b][:, COL_EXP:COL_EXP + 2], g_idx[b][:, 0:2]).then_inc(gexperts_ready, 1)
                past(dve, gexperts_ready, t)
                nc.vector.tensor_tensor(g_hot[b][:, :, :], row[b][:, COL_EXP:COL_EXP + 2].unsqueeze(2).to_broadcast([P, 2, NEXP]),
                                        eiota[:, :].unsqueeze(1).to_broadcast([P, 2, NEXP]), ALU.is_equal).then_inc(ghot_ready, 1)
                past(dve, ghot_ready, t)
                past(dve, pos_ready, t, 1)
                nc.vector.tensor_tensor(g_mask[b][:, :], g_hot[b][:, 0, :], g_hot[b][:, 1, :], ALU.add).then_inc(gmask_ready, 1)
                past(dve, gmask_ready, t)
                nc.vector.tensor_tensor(g_before[b + 1 - UNROLL][:, :], g_before[b][:, :], g_mask[b][:, :], ALU.add).then_inc(before_ready, 1)

            def slot_numbers(t, b):
                past(dve, pos_ready, t)
                nc.vector.tensor_tensor(g_over[b][:, :], slots_ps, elimit[:, :], ALU.is_ge).then_inc(over_ready, 1)
                past(dve, over_ready, t)
                nc.vector.scalar_tensor_tensor(out=g_slot8[b][:, :], in0=g_over[b][:, :], scalar=OUT_OF_TABLE,
                                               in1=slots_ps, op0=ALU.mult, op1=ALU.add).then_inc(slot8_ready, 1)
                past(dve, slot8_ready, t)
                nc.vector.tensor_tensor(g_sel[b][:, :, :], g_hot[b][:, :, :],
                                        g_slot8[b][:, :].unsqueeze(1).to_broadcast([P, 2, NEXP]), ALU.mult).then_inc(sel_ready, 1)
                past(dve, sel_ready, t)
                nc.vector.tensor_reduce(g_slotf[b][:, :], g_sel[b][:, :, :], AX_X, ALU.add).then_inc(slotf_ready, 1)
                past(dve, slotf_ready, t)
                nc.vector.tensor_copy(g_slot[b][:, :], g_slotf[b][:, :]).then_inc(slot_ready, 1)

            def step(i, u):
                if live(i, 7):
                    normalise2(i - 7, (u - 7) % UNROLL)
                if live(i, 5):
                    rms_sums(i - 5, (u - 5) % UNROLL)
                if live(i, 3):
                    scores(i - 3, (u - 3) % UNROLL)
                if live(i, 5):
                    rms_scale(i - 5, (u - 5) % UNROLL)
                if live(i, 9):
                    slot_numbers(i - 9, (u - 9) % UNROLL)
                if live(i, 3):
                    softmax(i - 3, (u - 3) % UNROLL)
                if live(i, 8):
                    gate_max(i - 8, (u - 8) % UNROLL)
                if live(i, 6):
                    add_attention(i - 6, (u - 6) % UNROLL)
                if live(i, 6):
                    past(dve, x1_ready, i - 6)
                if live(i, 1):
                    normalise1(i - 1, (u - 1) % UNROLL)
                if live(i, 6):
                    stats2(i - 6, (u - 6) % UNROLL)
                if live(i, 0):
                    stats1(i, u)
                    past(dve, ln1_stats, i)
                if live(i, 6):
                    past(dve, ln2_stats, i - 6)
                if live(i, 8):
                    gate_reciprocal(i - 8, (u - 8) % UNROLL)
                if live(i, 0):
                    aggregate1(i, u)
                if live(i, 6):
                    aggregate2(i - 6, (u - 6) % UNROLL)
                if live(i, 8):
                    route(i - 8, (u - 8) % UNROLL)

            run_tiles(dve, step)

            def chunk(e, c):
                n, b = e * NCH + c, c % 2
                dve.wait_ge(xe_loaded[b], (n // 2 + 1) * 16 if isinstance(n, int) else (e * (NCH // 2) + c // 2 + 1) * 16)
                past(dve, xeT_vector, n, 1)
                nc.vector.tensor_scalar(e_hit[b][:, :, :], xe[b][:, :, COL_EXP:COL_EXP + 2], e_now[:, :], None, ALU.is_equal).then_inc(hit_ready, 1)
                past(dve, hit_ready, n)
                nc.vector.tensor_tensor(e_w2[b][:, :, :], e_hit[b][:, :, :], xe[b][:, :, COL_W:COL_W + 2], ALU.mult).then_inc(wsel_ready, 1)
                past(dve, wsel_ready, n)
                past(dve, y_scaled, n, 2, CB)
                nc.vector.tensor_reduce(e_w[b][:, :], e_w2[b][:, :, :], AX_X, ALU.add).then_inc(wts_ready, 1)
                past(dve, y_added[b], e * (NCH // 2) + c // 2, 1, 16 * CB)
                nc.vector.tensor_copy(e_tok[b][:, :], xe[b][:, :, COL_TOK]).then_inc(toks_ready, 1)
                dve.wait_ge(xe_transposed, n * 2 + 2)
                past(dve, h_done, n, 2, 3)
                nc.vector.tensor_copy(xeT[b][:, 1, :], p2_xT[1][:, :, :].rearrange("p b q -> p (b q)")).then_inc(xeT_vector, 1)
                for j in range(FF // P):
                    m = n * 3 + j
                    past(dve, silu_done, m)
                    if j == 0:
                        past(dve, y_done, n, 2, 2)
                    q = (c * 3 + j) % 2
                    nc.vector.tensor_tensor(hT[b][:, j, :], silu[q][:, :], p2_h[q][1][:, :, :].rearrange("p b q -> p (b q)"),
                                            ALU.mult).then_inc(h_ready, 1)

            def next_expert(e):
                dve.wait_ge(hit_ready, (e + 1) * NCH)
                nc.vector.tensor_scalar(e_now[:, :], e_now[:, :], 1.0, None, ALU.add).then_inc(e_number, 1)
                dve.wait_ge(e_number, e + 2)

            for c in range(NCH):
                chunk(0, c)
            next_expert(0)
            with dve.Fori(1, NEXP) as e:
                for c in range(NCH):
                    chunk(e, c)
                next_expert(e)


_INS = ['L0_attn_x', 'L0_attn_Wq', 'L0_attn_Wk', 'L0_attn_Wv', 'L0_attn_Wo', 'L0_attn_lambda_q1', 'L0_attn_lambda_k1',
        'L0_attn_lambda_q2', 'L0_attn_lambda_k2', 'L0_attn_ln_w', 'L0_attn_ln_b', 'L0_ffn_w_gate', 'L0_ffn_c_fc',
        'L0_ffn_c_proj']


def kernel(**inputs):
    import numpy as _np
    import concourse.bacc as _bacc
    from concourse import mybir as _mybir
    from concourse.bass_utils import run_bass_kernel_spmd as _run

    nc = _bacc.Bacc("TRN2", target_bir_lowering=False, num_devices=1)
    arrays, args = {}, []
    for name in _INS:
        a = _np.ascontiguousarray(inputs[name])
        arrays[f"in_{name}_dram"] = a
        args.append(nc.dram_tensor(f"in_{name}_dram", a.shape, _mybir.dt.from_np(a.dtype), kind="ExternalInput").ap())
    b, s, e = inputs["L0_attn_x"].shape
    args.append(nc.dram_tensor("out_0_dram", (b * s + CAP, e), _mybir.dt.float32, kind="ExternalOutput").ap())
    build_block(nc, *args)
    r = _run(nc, [arrays], core_ids=[0])
    return r.results[0]["out_0_dram"][:b * s].reshape(b, s, e)
```

```python
import math

import concourse.bass as bass
from concourse import mybir
from contextlib import ExitStack

P = 128
E = 256
H = 8
D = 16
DV = 2 * D
CAP = 1024
NEXP = 8
FF = 384
FOLD = 2
EPS_LN = 1e-5
EPS_RMS = 1e-8
LAMBDA_INIT = 0.8 - 0.6 * math.exp(-0.3 * 12)
SCORE_SCALE = 1.0 / D ** 0.25
COL_EXP, COL_W, COL_TOK, ROW = E, E + 2, E + 4, E + 8
OUT_OF_TABLE = float(1 << 20)
LN_EXP_SET = 6
GROUP = 4
UNROLL = 8
RMS_SCALE = math.sqrt(EPS_LN / (EPS_RMS * DV))

F32 = mybir.dt.float32
BF16 = mybir.dt.bfloat16
I32 = mybir.dt.int32
U32 = mybir.dt.uint32
ALU = mybir.AluOpType
ACT = mybir.ActivationFunctionType
AX_X = mybir.AxisListType.X


def build_block(nc, x, wq, wk, wv, wo, lq1, lk1, lq2, lk2, ln_w, ln_b, w_gate, c_fc, c_proj, out):
    NTOK = x.shape[0] * x.shape[1]
    NT = NTOK // P
    NBLK = CAP // P
    CB = 4
    NCH = NBLK // CB
    SLOTS = NEXP * CAP
    x_rows = x.rearrange("b s e -> (b s) e")
    table = nc.dram_tensor("slot_table", [SLOTS, ROW], F32, kind="Internal").ap()

    with ExitStack() as ctx:
        def sb(name, shape, dt=F32):
            return ctx.enter_context(nc.sbuf_tensor(name, shape, dt))

        def pb(name, shape, dt=F32):
            return ctx.enter_context(nc.psum_tensor(name, shape, dt))

        def sem(name):
            return ctx.enter_context(nc.semaphore(name))

        x_all = sb("x_all", [P, NT, E])
        wqkv = sb("wqkv", [P, 2, 3 * E])
        wo_sb = sb("wo_sb", [P, 2, E])
        wg_sb = sb("wg_sb", [P, 2, NEXP])
        ident = sb("ident", [P, P])
        tri = sb("tri", [P, P], BF16)
        ones = sb("ones", [P, P], BF16)
        ebase = sb("ebase", [1, NEXP], BF16)
        elimit = sb("elimit", [P, NEXP])
        eiota = sb("eiota", [P, NEXP])
        tok_all = sb("tok_all", [P, NT])
        lam_in = sb("lam_in", [P, 2, 2, D])
        lam_prod = sb("lam_prod", [P, 2, D])
        lam_sum = sb("lam_sum", [P, 2])
        lam_exp = sb("lam_exp", [P, 2])
        neg_lam = sb("neg_lam", [P, 1])
        lnwb = sb("lnwb", [P, 2])
        lnwb_s = sb("lnwb_s", [P, 2])
        eps_ln = sb("eps_ln", [P, 1])
        fill = sb("fill", [P, NBLK, ROW])
        zeros = sb("zeros", [P, NBLK, E])
        two = range(2)

        def pair(name, shape, dt=F32):
            return [sb(f"{name}{b}", shape, dt) for b in two] * (UNROLL // 2)

        stat = pair("stat", [P, H + 2, 2])
        stat_ln = pair("stat_ln", [P, H + 2])
        rstd = pair("rstd", [P, H + 2])
        neg_mr = pair("neg_mr", [P, 2])
        bn1, bn2 = pair("bn1", [P, 6]), pair("bn2", [P, 6])
        xn = pair("xn", [P, E])
        xT = pair("xT", [P, 2, P])
        k_sb, v_sb = pair("k_sb", [P, E]), pair("v_sb", [P, E])
        qk_prod = sb("qk_prod", [P, H * H * 2 * D])
        s_raw = pair("s_raw", [P, H, H, 2])
        s_max = pair("s_max", [P, H, 2])
        s_sub = pair("s_sub", [P, 2, H, H])
        probs = pair("probs", [P, 2, H, H])
        p_sum, p_rec = pair("p_sum", [P, 2 * H]), pair("p_rec", [P, 2 * H])
        p_norm = pair("p_norm", [P, 2, H, H])
        w_att = pair("w_att", [P, H, H])
        v_prod = pair("v_prod", [P, H, H, DV])
        a_sb = pair("a_sb", [P, E])
        a_sq = pair("a_sq", [P, H, DV])
        a_n = pair("a_n", [P, E])
        aT = pair("aT", [P, 2, P])
        rows = sb("rows", [P, UNROLL, ROW])
        x2T = pair("x2T", [P, 2, P])
        g_max = pair("g_max", [P, GROUP])
        g_sub, g_exp = pair("g_sub", [P, GROUP, NEXP]), pair("g_exp", [P, GROUP, NEXP])
        g_sum, g_rec = pair("g_sum", [P, GROUP]), pair("g_rec", [P, GROUP])
        g_top, g_idx = pair("g_top", [P, GROUP, 8]), pair("g_idx", [P, GROUP, 8], U32)
        g_hot = pair("g_hot", [P, GROUP, 2, NEXP])
        g_mask = pair("g_mask", [P, GROUP, NEXP], BF16)
        g_count = pair("g_count", [P, NEXP])
        g_before = pair("g_before", [P, NEXP], BF16)
        g_over, g_slot8 = pair("g_over", [P, GROUP, NEXP]), pair("g_slot8", [P, GROUP, NEXP])
        g_sel = pair("g_sel", [P, GROUP, 2, NEXP])
        g_slotf, g_slot = pair("g_slotf", [P, GROUP, 2]), pair("g_slot", [P, GROUP, 2], I32)
        w1 = [sb(f"w1{b}", [P, 2, 2 * FF]) for b in two]
        w2 = [sb(f"w2{b}", [P, FF // P, E]) for b in two]
        xe = [sb(f"xe{b}", [P, CB, ROW]) for b in two]
        xeT = [sb(f"xeT{b}", [P, 2, CB * P]) for b in two]
        e_now = sb("e_now", [P, 1])
        e_hit = [sb(f"e_hit{b}", [P, CB, 2]) for b in two]
        e_w2 = [sb(f"e_w2{b}", [P, CB, 2]) for b in two]
        e_w = [sb(f"e_w{b}", [P, CB]) for b in two]
        e_tok = [sb(f"e_tok{b}", [P, CB], I32) for b in two]
        silu = [sb(f"silu{b}", [P, CB * P]) for b in two]
        hT = [sb(f"hT{b}", [P, FF // P, CB * P]) for b in two]
        y_sb = [sb(f"y_sb{b}", [P, CB, E]) for b in two]

        bank_t = pb("bank_t", [P, 4, P])
        bank_t2 = pb("bank_t2", [P, 4, P])
        bank_qk = [pb(f"bank_qk{b}", [P, 2, E]) for b in two] * (UNROLL // 2)
        bank_v = pb("bank_v", [P, 2, E])
        bank_a = pb("bank_a", [P, 2, E])
        bank_wo = pb("bank_wo", [P, 2, E])
        bank_g = pb("bank_g", [P, 2, E])
        logits = bank_g[:, 0, 0:GROUP * NEXP].rearrange("p (j e) -> p j e", e=NEXP)
        slots_ps = bank_g[:, 1, 0:GROUP * NEXP].rearrange("p (j e) -> p j e", e=NEXP)
        p2_xT = [bank_t, bank_t2]
        p2_h = [[bank_qk[0], bank_qk[1]], [bank_v, bank_a]]
        p2_y = [bank_wo, bank_g]

        x_loaded = [sem(f"x_loaded{c}") for c in range(4)]
        w_loaded = sem("w_loaded")
        consts = sem("consts")
        pool_chain = sem("pool_chain")
        lam_chain = sem("lam_chain")
        lam_ready = sem("lam_ready")
        filled = sem("filled")
        ln1_stats, ln1_aggr, ln2_stats, ln2_aggr, stat_log, rstd_ready, neg_mr_ready, xn_ready, xn2_ready = (
            sem(n) for n in "ln1_stats ln1_aggr ln2_stats ln2_aggr stat_log rstd_ready neg_mr_ready xn_ready xn2_ready".split())
        xn_transposed, xT_copied, qkv_done, k_copied, v_copied, qk_multiplied = (
            sem(n) for n in "xn_transposed xT_copied qkv_done k_copied v_copied qk_multiplied".split())
        scores_ready, smax_ready, ssub_ready, exp_done, psum_ready, prec_ready, pnorm_ready, w_ready, multiplied, products_ready = (
            sem(n) for n in "scores_ready smax_ready ssub_ready exp_done psum_ready prec_ready pnorm_ready w_ready multiplied products_ready".split())
        a_summed, a_copied, sq_done, ms_ready, an_ready, an_transposed, aT_copied, wo_done, x1_ready = (
            sem(n) for n in "a_summed a_copied sq_done ms_ready an_ready an_transposed aT_copied wo_done x1_ready".split())
        xn2_transposed, x2T_copied, logits_ready = (
            sem(n) for n in "xn2_transposed x2T_copied logits_ready".split())
        gmax_ready, gsub_ready, gexp_done, gsum_ready, gtop_ready, grec_ready, gidx_ready = (
            sem(n) for n in "gmax_ready gsub_ready gexp_done gsum_ready gtop_ready grec_ready gidx_ready".split())
        gweights_ready, gexperts_ready, gtokens_ready, ghot_ready, gmask_ready, gcount_ready, before_ready, pos_ready = (
            sem(n) for n in "gweights_ready gexperts_ready gtokens_ready ghot_ready gmask_ready gcount_ready before_ready pos_ready".split())
        over_ready, slot8_ready, sel_ready, slotf_ready, slot_ready = (
            sem(n) for n in "over_ready slot8_ready sel_ready slotf_ready slot_ready".split())
        scattered = [sem(f"scattered{r}") for r in range(UNROLL)]
        x1_stored = sem("x1_stored")
        e_loaded = [sem(f"e_loaded{b}") for b in two]
        xe_loaded = [sem(f"xe_loaded{b}") for b in two]
        e_number = sem("e_number")
        hit_ready, wsel_ready, wts_ready, toks_ready = sem("hit_ready"), sem("wsel_ready"), sem("wts_ready"), sem("toks_ready")
        xe_transposed = sem("xe_transposed")
        xeT_scalar, xeT_vector = sem("xeT_scalar"), sem("xeT_vector")
        h_done = sem("h_done")
        silu_done, h_ready = sem("silu_done"), sem("h_ready")
        y_done = sem("y_done")
        y_scaled = sem("y_scaled")
        y_added = [sem(f"y_added{b}") for b in two]

        def past(eng, s, t, back=0, per=1):
            if isinstance(t, int):
                if t - back < 0:
                    return
            eng.wait_ge(s, (t - (back - 1)) * per)

        LAG_MAX = 14
        FIRST = 2 * UNROLL

        def row_free(eng, t, r):
            if isinstance(t, int) and t < UNROLL:
                return
            eng.wait_ge(scattered[r], (t - r) * (32 // UNROLL))

        def run_tiles(eng, step):
            for i in range(FIRST):
                step(i, i % UNROLL, i // GROUP)
            with eng.Fori(0, (NT - FIRST) // UNROLL) as turn:
                for u in range(UNROLL):
                    step(turn * UNROLL + (FIRST + u), u, turn * (UNROLL // GROUP) + (FIRST + u) // GROUP)
            for i in range(NT, NT + LAG_MAX):
                step(i, i % UNROLL, i // GROUP)

        def live(i, lag):
            return not isinstance(i, int) or 0 <= i - lag < NT

        def group_live(q):
            return not isinstance(q, int) or 0 <= q - 3 < NT // GROUP

        def upto(eng, s, t, back=0):
            past(eng, s, min(t, NT - 1) if isinstance(t, int) else t, back)

        def x_tile(t):
            if isinstance(t, int):
                return x_all[:, t, :]
            return x_all[:, bass.ds(t, 1), :].rearrange("p a e -> p (a e)")

        W_LOADS = 16 * (3 + 4 + 2 * (P // DV) + 2)

        block = ctx.enter_context(nc.Block())

        @block.sync
        def _(sp):
            xv = x_rows.rearrange("(t p) e -> p t e", p=P)
            parts = [(0, 2), (2, 6), (6, 14), (14, NT)]
            sp.dma_start(x_all[:, 0:2, :], xv[:, 0:2, :]).then_inc(x_loaded[0], 16)
            for j, w in enumerate((wq, wk, wv)):
                sp.dma_start(wqkv[:, :, j * E:(j + 1) * E], w.rearrange("(k p) n -> p k n", p=P)).then_inc(w_loaded, 16)
            sp.wait_ge(w_loaded, W_LOADS)
            for c in range(1, 4):
                a, b = parts[c]
                sp.dma_start(x_all[:, a:b, :], xv[:, a:b, :]).then_inc(x_loaded[c], 16)
            sp.wait_ge(consts, 1)
            for e in range(NEXP):
                sp.dma_start(table[e * CAP:(e + 1) * CAP, :].rearrange("(b p) w -> p b w", p=P), fill[:, :, :]).then_inc(filled, 16)
            sp.dma_start(out[NTOK:NTOK + CAP, :].rearrange("(b p) w -> p b w", p=P), zeros[:, :, :]).then_inc(filled, 16)
            for e in range(2):
                sp.dma_start(w1[e][:, :, :], c_fc[e].rearrange("(k p) f -> p k f", p=P)).then_inc(e_loaded[e], 16)
                sp.dma_start(w2[e][:, :, :], c_proj[e].rearrange("(k p) n -> p k n", p=P)).then_inc(e_loaded[e], 16)
            ov = out[0:NTOK, :].rearrange("(t p) e -> p t e", p=P)
            for c in range(NT // 8):
                sp.wait_ge(x1_ready, 8 * (c + 1))
                sp.dma_start(ov[:, 8 * c:8 * c + 8, :], x_all[:, 8 * c:8 * c + 8, :]).then_inc(x1_stored, 16)
            for r in range(UNROLL):
                sp.wait_ge(scattered[r], 32 * NT // UNROLL)
            sp.wait_ge(filled, 16 * (NEXP + 1))

            def load_chunk(e, c, b):
                n = e * NCH + c
                past(sp, xe_transposed, n, 2, 2)
                past(sp, hit_ready, n, 2)
                past(sp, wsel_ready, n, 2)
                past(sp, toks_ready, n, 2)
                src = table.rearrange("(n b p) w -> n p b w", b=CB, p=P)
                s = src[n] if isinstance(n, int) else src[bass.ds(n, 1)].rearrange("n p b w -> (n p) b w")
                sp.dma_start(xe[b][:, :, :], s).then_inc(xe_loaded[b], 16)

            def load_expert(e, b):
                past(sp, y_done, e, 2, 2 * NCH)
                c1, c2 = c_fc, c_proj
                s1 = c1[bass.ds(e, 1)].rearrange("a (k p) f -> p (a k) f", p=P)
                s2 = c2[bass.ds(e, 1)].rearrange("a (k p) f -> p (a k) f", p=P)
                sp.dma_start(w1[b][:, :, :], s1).then_inc(e_loaded[b], 16)
                sp.dma_start(w2[b][:, :, :], s2).then_inc(e_loaded[b], 16)

            for e in range(2):
                for c in range(NCH):
                    load_chunk(e, c, c % 2)
            with sp.Fori(1, NEXP // 2) as h:
                for u in range(2):
                    load_expert(h * 2 + u, u)
                    for c in range(NCH):
                        load_chunk(h * 2 + u, c, c % 2)

        @block.gpsimd
        def _(pool):
            n = 0

            def chain(ins):
                nonlocal n
                ins.then_inc(pool_chain, 1)
                n += 1

            chain(pool.memset(ident[:, :], 0.0))
            pool.wait_ge(pool_chain, n)
            chain(pool.affine_select(out=ident[:, :], in_=ident[:, :], compare_op=ALU.not_equal, fill=1.0, base=0,
                                     pattern=[[-1, P]], channel_multiplier=1))
            chain(pool.memset(fill[:, :, :], 0.0))
            chain(pool.memset(zeros[:, :, :], 0.0))
            chain(pool.memset(ones[:, :], 1.0))
            chain(pool.memset(eps_ln[:, :], EPS_LN))
            pool.wait_ge(pool_chain, n)
            chain(pool.iota(fill[:, :, COL_TOK], pattern=[[P, NBLK]], base=NTOK, channel_multiplier=1,
                            allow_small_or_imprecise_dtypes=True))
            pool.wait_ge(pool_chain, n)
            pool.nop().then_inc(consts, 1)
            for i, (t, step, base) in enumerate(((eiota, 1, 0), (elimit, CAP, CAP))):
                chain(pool.iota(t[:, :], pattern=[[step, NEXP]], base=base, channel_multiplier=0,
                                allow_small_or_imprecise_dtypes=True))
            chain(pool.iota(ebase[:, :], pattern=[[CAP, NEXP]], base=0, channel_multiplier=0,
                            allow_small_or_imprecise_dtypes=True))
            chain(pool.iota(tok_all[:, :], pattern=[[P, NT]], base=0, channel_multiplier=1,
                            allow_small_or_imprecise_dtypes=True))
            chain(pool.affine_select(out=tri[:, :], in_=ones[:, :], compare_op=ALU.is_gt, fill=0.0, base=0,
                                     pattern=[[1, P]], channel_multiplier=-1))
            chain(pool.memset(rows[:, :, :], 0.0))
            for b in two:
                chain(pool.memset(stat[b][:, :, :], 1.0))
            chain(pool.memset(g_before[0][:, :], 0.0))
            pool.wait_ge(pool_chain, n)
            pool.nop().then_inc(consts, 1)

            def products(t, b):
                past(pool, w_ready, t)
                past(pool, v_copied, t)
                past(pool, a_summed, t, 2)
                pool.tensor_tensor(
                    v_prod[b][:, :, :, :],
                    w_att[b][:, :, :].rearrange("p n m -> p m n").unsqueeze(3).to_broadcast([P, H, H, DV]),
                    v_sb[b][:, :].rearrange("p (m e) -> p m e", m=H).unsqueeze(2).to_broadcast([P, H, H, DV]),
                    ALU.mult).then_inc(multiplied, 1)
                past(pool, multiplied, t)
                pool.tensor_tensor(v_prod[b][:, 0:FOLD, :, :].rearrange("p m n e -> p (m n e)"),
                                   v_prod[b][:, 0:FOLD, :, :].rearrange("p m n e -> p (m n e)"),
                                   v_prod[b][:, H - FOLD:, :, :].rearrange("p m n e -> p (m n e)"),
                                   ALU.add).then_inc(products_ready, 1)

            def rms_scale(t, b, u):
                past(pool, rstd_ready, t, -6)
                past(pool, a_copied, t)
                past(pool, an_transposed, t, 2)
                pool.tensor_tensor(a_n[b][:, :].rearrange("p (n e) -> p n e", n=H),
                                   a_sb[b][:, :].rearrange("p (n e) -> p n e", n=H),
                                   rstd[u][:, 0:H].unsqueeze(2).to_broadcast([P, H, DV]),
                                   ALU.mult).then_inc(an_ready, 1)

            def row_waits(g):
                past(pool, slot_ready, g)
                past(pool, gweights_ready, g)
                past(pool, gexperts_ready, g)
                past(pool, gtokens_ready, g)
                if isinstance(g, int) and g == 0:
                    pool.wait_ge(filled, 16 * (NEXP + 1))

            def scatter(t, r):
                gb, j = r // GROUP, r % GROUP
                for k in range(2):
                    pool.indirect_dma_start(
                        out=table, out_offset=bass.IndirectOffsetOnAxis(ap=g_slot[gb][:, j, k:k + 1], axis=0),
                        in_=rows[:, r, :], in_offset=None, bounds_check=SLOTS - 1, oob_is_err=False,
                    ).then_inc(scattered[r], 16)

            def step(i, u, q):
                if live(i, 6):
                    rms_scale(i - 6, (u - 6) % UNROLL, u)
                if live(i, 14):
                    past(pool, xn2_ready, i - 14)
                    if u % GROUP == 2:
                        row_waits(q - 3)
                if live(i, 3):
                    products(i - 3, (u - 3) % UNROLL)
                if live(i, 14):
                    scatter(i - 14, (u - 14) % UNROLL)

            run_tiles(pool, step)

            pool.wait_ge(x1_stored, 16 * (NT // 8))

            def add_chunk(e, c):
                n = e * NCH + c
                past(pool, toks_ready, n)
                if c == 0:
                    for b in two:
                        pool.wait_ge(y_added[b], 16 * CB * (NCH // 2) * e)
                for k in range(CB):
                    pool.wait_ge(y_scaled, n * CB + k + 1)
                    pool.indirect_dma_start(
                        out=out, out_offset=bass.IndirectOffsetOnAxis(ap=e_tok[c % 2][:, k:k + 1], axis=0),
                        in_=y_sb[c % 2][:, k, :], in_offset=None, compute_op=ALU.add,
                    ).then_inc(y_added[c % 2], 16)

            for e in range(NEXP):
                for c in range(NCH):
                    add_chunk(e, c)
            for b in two:
                pool.wait_ge(y_added[b], 16 * CB * (NCH // 2) * NEXP)

        @block.scalar
        def _(act):
            act.dma_start(lam_in[:, 0, 0, :], lq1.rearrange("(a d) -> a d", a=1).to_broadcast([P, D])).then_inc(w_loaded, 16)
            act.dma_start(lam_in[:, 0, 1, :], lk1.rearrange("(a d) -> a d", a=1).to_broadcast([P, D])).then_inc(w_loaded, 16)
            act.dma_start(lam_in[:, 1, 0, :], lq2.rearrange("(a d) -> a d", a=1).to_broadcast([P, D])).then_inc(w_loaded, 16)
            act.dma_start(lam_in[:, 1, 1, :], lk2.rearrange("(a d) -> a d", a=1).to_broadcast([P, D])).then_inc(w_loaded, 16)
            for r in range(P // DV):
                act.dma_start(lnwb[r * DV:(r + 1) * DV, 0:1], ln_w.rearrange("(d a) -> d a", a=1)).then_inc(w_loaded, 16)
                act.dma_start(lnwb[r * DV:(r + 1) * DV, 1:2], ln_b.rearrange("(d a) -> d a", a=1)).then_inc(w_loaded, 16)
            act.dma_start(wo_sb[:, :, :], wo.rearrange("(k p) n -> p k n", p=P)).then_inc(w_loaded, 16)
            act.dma_start(wg_sb[:, :, :], w_gate.rearrange("(k p) n -> p k n", p=P)).then_inc(w_loaded, 16)
            act.add_instruction(mybir.InstLoadActFuncSet(name=nc.get_next_instruction_name(), ins=[], outs=[], act_func_set_id=LN_EXP_SET))
            act.wait_ge(lam_chain, 2)
            act.wait_ge(consts, 2)
            nc.scalar.activation(lam_exp[:, :], lam_sum[:, :], ACT.Exp).then_inc(lam_ready, 1)

            def copy_xT(t, b):
                past(act, xn_transposed, t)
                past(act, qkv_done, t, 2)
                nc.scalar.copy(xT[b][:, :, :], bank_t[:, 0:2, :]).then_inc(xT_copied, 1)

            def copy_kv(t, b):
                past(act, qkv_done, t)
                past(act, qk_multiplied, t, 2)
                nc.scalar.copy(k_sb[b][:, :], bank_qk[b][:, 1, :]).then_inc(k_copied, 1)
                past(act, products_ready, t, 2)
                nc.scalar.copy(v_sb[b][:, :], bank_v[:, 0, :]).then_inc(v_copied, 1)

            def exp_scores(t, b):
                past(act, ssub_ready, t)
                past(act, pnorm_ready, t, 2)
                nc.scalar.activation(probs[b][:, :, :, :], s_sub[b][:, :, :, :], ACT.Exp, scale=SCORE_SCALE).then_inc(exp_done, 1)

            def copy_a(t, b):
                past(act, a_summed, t)
                past(act, an_ready, t, 2)
                nc.scalar.copy(a_sb[b][:, :], bank_a[:, 0, :]).then_inc(a_copied, 1)

            def square(t, b):
                past(act, a_copied, t)
                past(act, ms_ready, t, 2)
                nc.scalar.activation(a_sq[b][:, :, :].rearrange("p n e -> p (n e)"), a_sb[b][:, :], ACT.Square,
                                     scale=RMS_SCALE).then_inc(sq_done, 1)

            def copy_aT(t, b):
                if isinstance(t, int) and t == 0:
                    act.wait_ge(lam_ready, 3)
                past(act, an_transposed, t)
                if live(t + 7, 9):
                    upto(act, xn2_transposed, t, 2)
                past(act, wo_done, t, 2)
                nc.scalar.activation(aT[b][:, :, :], bank_t2[:, 2:4, :], ACT.Identity, bias=lnwb_s[:, 1:2],
                                     scale=lnwb_s[:, 0:1]).then_inc(aT_copied, 1)

            def copy_x2T(t, b):
                past(act, xn2_transposed, t)
                past(act, logits_ready, t, 2)
                nc.scalar.copy(x2T[b][:, :, :], bank_t2[:, 0:2, :]).then_inc(x2T_copied, 1)

            def exp_gate(g, gb):
                past(act, gsub_ready, g)
                past(act, gidx_ready, g, 2)
                past(act, gsum_ready, g, 2)
                nc.scalar.activation(g_exp[gb][:, :, :], g_sub[gb][:, :, :], ACT.Exp).then_inc(gexp_done, 1)

            def roots(i, u):
                if live(i, 1):
                    past(act, ln1_aggr, i - 1)
                if live(i, 6):
                    past(act, ms_ready, i - 6)
                if live(i, 8):
                    past(act, ln2_aggr, i - 8)
                nc.scalar.activation(stat_ln[u][:, :], stat[u][:, :, 1], ACT.Ln, bias=eps_ln[:, :]).then_inc(stat_log, 1)
                past(act, stat_log, i)
                past(act, neg_mr_ready, i, 2)
                if live(i, 8):
                    past(act, an_ready, i - 8)
                nc.scalar.activation(rstd[u][:, :], stat_ln[u][:, :], ACT.Exp, scale=-0.5).then_inc(rstd_ready, 1)

            def normalise_waits(i, u):
                past(act, neg_mr_ready, i)
                if live(i, 1):
                    past(act, xn_transposed, i - 1, 2)
                if live(i, 8):
                    row_free(act, i - 8, (u - 8) % UNROLL)

            def normalise1(t, u):
                nc.scalar.activation(xn[(u - 1) % UNROLL][:, :], x_tile(t), ACT.Identity, bias=neg_mr[u][:, 0:1],
                                     scale=rstd[u][:, H:H + 1]).then_inc(xn_ready, 1)

            def normalise2(t, u, r):
                nc.scalar.activation(rows[:, r, 0:E], x_tile(t), ACT.Identity, bias=neg_mr[u][:, 1:2],
                                     scale=rstd[u][:, H + 1:H + 2]).then_inc(xn2_ready, 1)

            def step(i, u, q):
                if live(i, 7):
                    copy_aT(i - 7, (u - 7) % UNROLL)
                if live(i, 9):
                    copy_x2T(i - 9, (u - 9) % UNROLL)
                if live(i, 5):
                    copy_a(i - 5, (u - 5) % UNROLL)
                if u % GROUP == 1 and group_live(q):
                    exp_gate(q - 3, (u // GROUP - 3) % 2)
                roots(i, u)
                if live(i, 5):
                    square(i - 5, (u - 5) % UNROLL)
                if live(i, 2):
                    copy_kv(i - 2, (u - 2) % UNROLL)
                normalise_waits(i, u)
                if live(i, 3):
                    exp_scores(i - 3, (u - 3) % UNROLL)
                if live(i, 1):
                    normalise1(i - 1, u)
                if live(i, 8):
                    normalise2(i - 8, u, (u - 8) % UNROLL)
                if live(i, 1):
                    copy_xT(i - 1, (u - 1) % UNROLL)

            run_tiles(act, step)

            def chunk(e, c):
                n, b = e * NCH + c, c % 2
                act.wait_ge(xe_transposed, n * 2 + 1)
                past(act, h_done, n, 2, 3)
                nc.scalar.copy(xeT[b][:, 0, :], p2_xT[0][:, :, :].rearrange("p b q -> p (b q)")).then_inc(xeT_scalar, 1)
                for j in range(FF // P):
                    act.wait_ge(h_done, n * 3 + j + 1)
                    m = n * 3 + j
                    past(act, h_ready, m, 2)
                    q = (c * 3 + j) % 2
                    nc.scalar.activation(silu[q][:, :], p2_h[q][0][:, :, :].rearrange("p b q -> p (b q)"),
                                         ACT.Silu).then_inc(silu_done, 1)
                act.wait_ge(wts_ready, n + 1)
                for k in range(CB):
                    act.wait_ge(y_done, n * 2 + k // 2 + 1)
                    if k == 0:
                        past(act, y_added[b], e * (NCH // 2) + c // 2, 1, 16 * CB)
                    nc.scalar.activation(y_sb[b][:, k, :], p2_y[k // 2][:, k % 2, :], ACT.Copy, scale=e_w[b][:, k:k + 1]).then_inc(y_scaled, 1)

            for c in range(NCH):
                chunk(0, c)
            with act.Fori(1, NEXP) as e:
                for c in range(NCH):
                    chunk(e, c)

        @block.tensor
        def _(pe):
            pe.wait_ge(w_loaded, W_LOADS)
            pe.wait_ge(consts, 2)

            def transpose_x(t, b):
                past(pe, xn_ready, t)
                past(pe, xT_copied, t, 1)
                for k in range(2):
                    last = nc.tensor.transpose(bank_t[:, k, :], xn[b][:, k * P:(k + 1) * P], ident[:, :])
                last.then_inc(xn_transposed, 1)

            def project(t, b):
                past(pe, xT_copied, t)
                past(pe, qk_multiplied, t, 2)
                for k in range(2):
                    nc.tensor.matmul(bank_qk[b][:, :, :].rearrange("p a e -> p (a e)"), xT[b][:, k, :],
                                     wqkv[:, k, 0:2 * E], start=(k == 0), stop=(k == 1))
                past(pe, v_copied, t, 1)
                for k in range(2):
                    last = nc.tensor.matmul(bank_v[:, 0, :], xT[b][:, k, :], wqkv[:, k, 2 * E:3 * E],
                                            start=(k == 0), stop=(k == 1))
                last.then_inc(qkv_done, 1)

            def sum_heads(t, b):
                past(pe, products_ready, t)
                past(pe, a_copied, t, 1)
                for m in range(H - FOLD):
                    last = nc.tensor.matmul(bank_a[:, 0, :], ident[:, :],
                                            v_prod[b][:, m, :, :].rearrange("p n e -> p (n e)"),
                                            start=(m == 0), stop=(m == H - FOLD - 1))
                last.then_inc(a_summed, 1)

            def transpose_a(t, b):
                past(pe, an_ready, t)
                past(pe, aT_copied, t, 1)
                past(pe, x2T_copied, t, 3)
                for k in range(2):
                    last = nc.tensor.transpose(bank_t2[:, 2 + k, :], a_n[b][:, k * P:(k + 1) * P], ident[:, :])
                last.then_inc(an_transposed, 1)

            def out_project(t, b):
                past(pe, aT_copied, t)
                past(pe, x1_ready, t, 1)
                for k in range(2):
                    last = nc.tensor.matmul(bank_wo[:, 0, :], aT[b][:, k, :], wo_sb[:, k, :], start=(k == 0), stop=(k == 1))
                last.then_inc(wo_done, 1)

            def transpose_x2(t, r):
                past(pe, xn2_ready, t)
                past(pe, x2T_copied, t, 1)
                upto(pe, aT_copied, t + 1)
                for k in range(2):
                    last = nc.tensor.transpose(bank_t2[:, k, :], rows[:, r, k * P:(k + 1) * P], ident[:, :])
                last.then_inc(xn2_transposed, 1)

            def gate(t, r, q):
                past(pe, x2T_copied, t)
                j = r % GROUP
                if j == 0:
                    past(pe, gsub_ready, q - 3)
                if j == 1:
                    past(pe, slot8_ready, q - 3)
                for k in range(2):
                    last = nc.tensor.matmul(logits[:, j, :], x2T[r][:, k, :], wg_sb[:, k, :], start=(k == 0), stop=(k == 1))
                last.then_inc(logits_ready, 1)

            def positions(g, gb):
                past(pe, gmask_ready, g)
                past(pe, before_ready, g, 1)
                nc.tensor.matmul(slots_ps, tri[:, :], g_mask[gb][:, :, :], start=True, stop=False)
                nc.tensor.matmul(slots_ps, ones[:, :], g_before[gb][:, :].unsqueeze(1).to_broadcast([P, GROUP, NEXP]),
                                 start=False, stop=False)
                for j in range(GROUP - 1):
                    after = GROUP - 1 - j
                    nc.tensor.matmul(slots_ps[:, j + 1:, :], ones[:, :],
                                     g_mask[gb][:, j, :].unsqueeze(1).to_broadcast([P, after, NEXP]), start=False, stop=False)
                nc.tensor.matmul(slots_ps, ones[0:1, :], ebase[:, :].unsqueeze(1).to_broadcast([1, GROUP, NEXP]),
                                 start=False, stop=True).then_inc(pos_ready, 1)

            def step(i, u, q):
                if u % GROUP == 2 and group_live(q):
                    positions(q - 3, (u // GROUP - 3) % 2)
                if live(i, 7):
                    transpose_a(i - 7, (u - 7) % UNROLL)
                if live(i, 9):
                    transpose_x2(i - 9, (u - 9) % UNROLL)
                if live(i, 2):
                    project(i - 2, (u - 2) % UNROLL)
                if live(i, 7):
                    out_project(i - 7, (u - 7) % UNROLL)
                if live(i, 9):
                    gate(i - 9, (u - 9) % UNROLL, q)
                if live(i, 4):
                    sum_heads(i - 4, (u - 4) % UNROLL)
                if live(i, 1):
                    transpose_x(i - 1, (u - 1) % UNROLL)

            run_tiles(pe, step)

            pe.wait_ge(slot8_ready, NT // GROUP)
            pe.wait_ge(x2T_copied, NT)

            def chunk(e, c, wb):
                n, b = e * NCH + c, c % 2
                pe.wait_ge(xe_loaded[b], (n // 2 + 1) * 16 if isinstance(n, int) else (e * (NCH // 2) + c // 2 + 1) * 16)
                for k in range(2):
                    past(pe, (xeT_scalar, xeT_vector)[k], n, 1)
                    for q in range(CB):
                        last = nc.tensor.transpose(p2_xT[k][:, q, :], xe[b][:, q, k * P:(k + 1) * P], ident[:, :])
                    last.then_inc(xe_transposed, 1)
                pe.wait_ge(xeT_scalar, n + 1)
                pe.wait_ge(xeT_vector, n + 1)
                for j in range(FF // P):
                    m = n * 3 + j
                    past(pe, h_ready, m, 2)
                    q = (c * 3 + j) % 2
                    for half in range(2):
                        for k in range(2):
                            last = nc.tensor.matmul(
                                p2_h[q][half][:, :, :].rearrange("p b q -> p (b q)"),
                                w1[wb][:, k, half * FF + j * P:half * FF + (j + 1) * P], xeT[b][:, k, :],
                                start=(k == 0), stop=(k == 1))
                    last.then_inc(h_done, 1)
                pe.wait_ge(h_ready, n * 3 + 3)
                for k in range(CB):
                    if k % 2 == 0:
                        past(pe, y_scaled, n * CB + k + 1, CB)
                    for j in range(FF // P):
                        last = nc.tensor.matmul(p2_y[k // 2][:, k % 2, :], hT[b][:, j, k * P:(k + 1) * P], w2[wb][:, j, :],
                                                start=(j == 0), stop=(j == FF // P - 1))
                    if k % 2 == 1:
                        last.then_inc(y_done, 1)

            def expert(e, wb):
                pe.wait_ge(e_loaded[wb], (e // 2 + 1) * 32 if isinstance(e, int) else (e - wb) * 16 + 32)
                for c in range(NCH):
                    chunk(e, c, wb)

            for e in range(2):
                expert(e, e)
            with pe.Fori(1, NEXP // 2) as h:
                for u in range(2):
                    expert(h * 2 + u, u)

        @block.vector
        def _(dve):
            dve.wait_ge(w_loaded, W_LOADS)
            nc.vector.tensor_tensor(lam_prod[:, :, :], lam_in[:, :, 0, :], lam_in[:, :, 1, :], ALU.mult).then_inc(lam_chain, 1)
            dve.wait_ge(lam_chain, 1)
            nc.vector.tensor_reduce(lam_sum[:, :], lam_prod[:, :, :], AX_X, ALU.add).then_inc(lam_chain, 1)
            nc.vector.tensor_scalar(lnwb_s[:, 0:1], lnwb[:, 0:1], (1.0 - LAMBDA_INIT) * math.sqrt(DV) * RMS_SCALE, None, ALU.mult).then_inc(lam_ready, 1)
            nc.vector.tensor_scalar(lnwb_s[:, 1:2], lnwb[:, 1:2], 1.0 - LAMBDA_INIT, None, ALU.mult).then_inc(lam_ready, 1)
            dve.wait_ge(lam_ready, 3)
            nc.vector.tensor_tensor(neg_lam[:, :], lam_exp[:, 1:2], lam_exp[:, 0:1], ALU.subtract).then_inc(lam_chain, 1)
            dve.wait_ge(lam_chain, 3)
            nc.vector.tensor_scalar(neg_lam[:, :], neg_lam[:, :], LAMBDA_INIT, None, ALU.subtract).then_inc(lam_chain, 1)
            nc.vector.memset(e_now[:, :], 0.0).then_inc(e_number, 1)
            dve.wait_ge(lam_chain, 4)
            dve.wait_ge(consts, 2)
            arrive = {0: 0, 2: 1, 6: 2, 14: 3}

            def attention_added(t, b):
                past(dve, wo_done, t)
                nc.vector.tensor_tensor(x_tile(t), bank_wo[:, 0, :], x_tile(t), ALU.add).then_inc(x1_ready, 1)

            def score_products(t, b):
                past(dve, k_copied, t)
                past(dve, scores_ready, t, 1)
                q4 = bank_qk[b][:, 0, :].rearrange("p (n f) -> p n f", n=H).unsqueeze(2).to_broadcast([P, H, H, DV])
                k4 = k_sb[b][:, :].rearrange("p (m f) -> p m f", m=H).unsqueeze(1).to_broadcast([P, H, H, DV])
                nc.vector.tensor_tensor(qk_prod[:, :].rearrange("p (n m f) -> p n m f", n=H, m=H), q4, k4, ALU.mult).then_inc(qk_multiplied, 1)

            def score_sums(t, b):
                past(dve, qk_multiplied, t)
                nc.vector.tensor_reduce(s_raw[b][:, :, :, :].rearrange("p n m c -> p (n m c)"),
                                        qk_prod[:, :].rearrange("p (s d) -> p s d", d=D), AX_X, ALU.add).then_inc(scores_ready, 1)

            def score_max(t, b):
                past(dve, scores_ready, t)
                nc.vector.tensor_reduce(s_max[b][:, :, :], s_raw[b][:, :, :, :].rearrange("p n m c -> p n c m"),
                                        AX_X, ALU.max).then_inc(smax_ready, 1)

            def score_subtract(t, b):
                past(dve, smax_ready, t)
                past(dve, exp_done, t, 2)
                nc.vector.tensor_tensor(s_sub[b][:, :, :, :].rearrange("p c n m -> p n m c"), s_raw[b][:, :, :, :],
                                        s_max[b][:, :, :].unsqueeze(2).to_broadcast([P, H, H, 2]), ALU.subtract).then_inc(ssub_ready, 1)

            def prob_sum(t, b):
                past(dve, exp_done, t)
                nc.vector.tensor_reduce(p_sum[b][:, :], probs[b][:, :, :, :].rearrange("p c n m -> p (c n) m"),
                                        AX_X, ALU.add).then_inc(psum_ready, 1)

            def prob_reciprocal(t, b):
                past(dve, psum_ready, t)
                nc.vector.reciprocal(p_rec[b][:, :], p_sum[b][:, :]).then_inc(prec_ready, 1)

            def prob_normalise(t, b):
                past(dve, prec_ready, t)
                nc.vector.tensor_tensor(p_norm[b][:, :, :, :].rearrange("p c n m -> p (c n) m"),
                                        probs[b][:, :, :, :].rearrange("p c n m -> p (c n) m"),
                                        p_rec[b][:, :].unsqueeze(2).to_broadcast([P, 2 * H, H]), ALU.mult).then_inc(pnorm_ready, 1)

            def prob_difference(t, b):
                past(dve, pnorm_ready, t)
                past(dve, products_ready, t, 2)
                nc.vector.scalar_tensor_tensor(out=w_att[b][:, :, :].rearrange("p n m -> p (n m)"),
                                               in0=p_norm[b][:, 1, :, :].rearrange("p n m -> p (n m)"), scalar=neg_lam[:, :],
                                               in1=p_norm[b][:, 0, :, :].rearrange("p n m -> p (n m)"),
                                               op0=ALU.mult, op1=ALU.add).then_inc(w_ready, 1)

            def rms_sums(t, b, u):
                past(dve, sq_done, t)
                nc.vector.tensor_reduce(stat[(u + 1) % UNROLL][:, 0:H, 1], a_sq[b][:, :, :], AX_X, ALU.add).then_inc(ms_ready, 1)

            def mean_terms(i, u):
                past(dve, rstd_ready, i)
                if live(i, 3):
                    past(dve, xn_ready, i - 3)
                if live(i, 10):
                    past(dve, xn2_ready, i - 10)
                nc.vector.scalar_tensor_tensor(out=neg_mr[u][:, :], in0=stat[u][:, H:H + 2, 0], scalar=-1.0,
                                               in1=rstd[u][:, H:H + 2], op0=ALU.mult, op1=ALU.mult).then_inc(neg_mr_ready, 1)

            def gate_max(g, gb, i):
                past(dve, logits_ready, i - 10)
                nc.vector.tensor_reduce(g_max[gb][:, :], logits, AX_X, ALU.max).then_inc(gmax_ready, 1)

            def gate_subtract(g, gb):
                past(dve, gmax_ready, g)
                nc.vector.tensor_tensor(g_sub[gb][:, :, :], logits, g_max[gb][:, :].unsqueeze(2).to_broadcast([P, GROUP, NEXP]),
                                        ALU.subtract).then_inc(gsub_ready, 1)

            def gate_top(g, gb):
                past(dve, gexp_done, g)
                nc.vector.tensor_reduce(g_sum[gb][:, :], g_exp[gb][:, :, :], AX_X, ALU.add).then_inc(gsum_ready, 1)
                for j in range(GROUP):
                    last = nc.vector.max(g_top[gb][:, j, :], g_exp[gb][:, j, :])
                last.then_inc(gtop_ready, 1)

            def gate_indices(g, gb):
                past(dve, gsum_ready, g)
                past(dve, gtop_ready, g)
                nc.vector.reciprocal(g_rec[gb][:, :], g_sum[gb][:, :]).then_inc(grec_ready, 1)
                for j in range(GROUP):
                    last = nc.vector.max_index(g_idx[gb][:, j, :], g_top[gb][:, j, :], g_exp[gb][:, j, :])
                last.then_inc(gidx_ready, 1)

            def row_weights(g, gb):
                past(dve, grec_ready, g)
                nc.vector.tensor_tensor(rows[:, gb * GROUP:(gb + 1) * GROUP, COL_W:COL_W + 2], g_top[gb][:, :, 0:2],
                                        g_rec[gb][:, :].unsqueeze(2).to_broadcast([P, GROUP, 2]), ALU.mult).then_inc(gweights_ready, 1)

            def row_experts(g, gb):
                past(dve, gidx_ready, g)
                nc.vector.tensor_copy(rows[:, gb * GROUP:(gb + 1) * GROUP, COL_EXP:COL_EXP + 2],
                                      g_idx[gb][:, :, 0:2]).then_inc(gexperts_ready, 1)

            def row_tokens(g, gb, i):
                t0 = i - 13
                src = tok_all[:, t0:t0 + GROUP] if isinstance(i, int) else tok_all[:, bass.ds(t0, GROUP)]
                nc.vector.tensor_copy(rows[:, gb * GROUP:(gb + 1) * GROUP, COL_TOK], src).then_inc(gtokens_ready, 1)

            def expert_hot(g, gb):
                past(dve, gexperts_ready, g)
                nc.vector.tensor_tensor(
                    g_hot[gb][:, :, :, :],
                    rows[:, gb * GROUP:(gb + 1) * GROUP, COL_EXP:COL_EXP + 2].unsqueeze(3).to_broadcast([P, GROUP, 2, NEXP]),
                    eiota[:, :].unsqueeze(1).unsqueeze(1).to_broadcast([P, GROUP, 2, NEXP]), ALU.is_equal).then_inc(ghot_ready, 1)

            def expert_mask(g, gb):
                past(dve, ghot_ready, g)
                nc.vector.tensor_tensor(g_mask[gb][:, :, :], g_hot[gb][:, :, 0, :], g_hot[gb][:, :, 1, :], ALU.add).then_inc(gmask_ready, 1)

            def expert_count(g, gb):
                past(dve, gmask_ready, g)
                nc.vector.tensor_reduce(g_count[gb][:, :], g_mask[gb][:, :, :].rearrange("p j e -> p e j"), AX_X, ALU.add).then_inc(gcount_ready, 1)

            def expert_before(g, gb):
                past(dve, gcount_ready, g)
                past(dve, pos_ready, g, 1)
                nc.vector.tensor_tensor(g_before[gb + 1][:, :], g_before[gb][:, :], g_count[gb][:, :], ALU.add).then_inc(before_ready, 1)

            def slot_over(g, gb):
                past(dve, pos_ready, g)
                nc.vector.tensor_tensor(g_over[gb][:, :, :], slots_ps, elimit[:, :].unsqueeze(1).to_broadcast([P, GROUP, NEXP]),
                                        ALU.is_ge).then_inc(over_ready, 1)

            def slot_pushed(g, gb):
                past(dve, over_ready, g)
                nc.vector.scalar_tensor_tensor(out=g_slot8[gb][:, :, :], in0=g_over[gb][:, :, :], scalar=OUT_OF_TABLE,
                                               in1=slots_ps, op0=ALU.mult, op1=ALU.add).then_inc(slot8_ready, 1)

            def slot_select(g, gb):
                past(dve, slot8_ready, g)
                nc.vector.tensor_tensor(g_sel[gb][:, :, :, :], g_hot[gb][:, :, :, :],
                                        g_slot8[gb][:, :, :].unsqueeze(2).to_broadcast([P, GROUP, 2, NEXP]), ALU.mult).then_inc(sel_ready, 1)

            def slot_sum(g, gb):
                past(dve, sel_ready, g)
                nc.vector.tensor_reduce(g_slotf[gb][:, :, :], g_sel[gb][:, :, :, :], AX_X, ALU.add).then_inc(slotf_ready, 1)

            def slot_integer(g, gb):
                past(dve, slotf_ready, g)
                nc.vector.tensor_copy(g_slot[gb][:, :, :], g_slotf[gb][:, :, :]).then_inc(slot_ready, 1)

            def step(i, u, q):
                routes = u % GROUP == 1 and group_live(q)
                slots = u % GROUP == 2 and group_live(q)
                g, gb = q - 3, (u // GROUP - 3) % 2
                b3 = (u - 3) % UNROLL
                if routes:
                    gate_max(g, gb, i)
                if live(i, 1):
                    past(dve, ln1_stats, i - 1)
                if live(i, 8):
                    past(dve, ln2_stats, i - 8)
                if live(i, 3):
                    score_products(i - 3, b3)
                if routes:
                    gate_subtract(g, gb)
                if slots:
                    slot_over(g, gb)
                if live(i, 1):
                    nc.vector.bn_aggr(stat[u][:, H, :], bn1[(u - 1) % UNROLL][:, :]).then_inc(ln1_aggr, 1)
                if live(i, 8):
                    nc.vector.bn_aggr(stat[u][:, H + 1, :], bn2[u][:, :]).then_inc(ln2_aggr, 1)
                if live(i, 3):
                    score_sums(i - 3, b3)
                if slots:
                    slot_pushed(g, gb)
                if routes:
                    gate_top(g, gb)
                mean_terms(i, u)
                if live(i, 3):
                    score_max(i - 3, b3)
                if live(i, 5):
                    rms_sums(i - 5, (u - 5) % UNROLL, u)
                if slots:
                    slot_select(g, gb)
                if live(i, 3):
                    score_subtract(i - 3, b3)
                if live(i, 7):
                    attention_added(i - 7, (u - 7) % UNROLL)
                if routes:
                    gate_indices(g, gb)
                if slots:
                    slot_sum(g, gb)
                if live(i, 3):
                    prob_sum(i - 3, b3)
                if routes:
                    row_weights(g, gb)
                    row_experts(g, gb)
                    row_tokens(g, gb, i)
                if live(i, 0):
                    if isinstance(i, int) and i in arrive:
                        dve.wait_ge(x_loaded[arrive[i]], 16)
                    nc.vector.bn_stats(bn1[u][:, :], x_tile(i)).then_inc(ln1_stats, 1)
                if live(i, 7):
                    past(dve, x1_ready, i - 7)
                if live(i, 3):
                    prob_reciprocal(i - 3, b3)
                if routes:
                    expert_hot(g, gb)
                if slots:
                    slot_integer(g, gb)
                if live(i, 7):
                    nc.vector.bn_stats(bn2[(u + 1) % UNROLL][:, :], x_tile(i - 7)).then_inc(ln2_stats, 1)
                if routes:
                    expert_mask(g, gb)
                if live(i, 3):
                    prob_normalise(i - 3, b3)
                if routes:
                    expert_count(g, gb)
                if live(i, 3):
                    prob_difference(i - 3, b3)
                if routes:
                    expert_before(g, gb)

            run_tiles(dve, step)

            def chunk(e, c):
                n, b = e * NCH + c, c % 2
                dve.wait_ge(xe_loaded[b], (n // 2 + 1) * 16 if isinstance(n, int) else (e * (NCH // 2) + c // 2 + 1) * 16)
                past(dve, xeT_vector, n, 1)
                nc.vector.tensor_scalar(e_hit[b][:, :, :], xe[b][:, :, COL_EXP:COL_EXP + 2], e_now[:, :], None, ALU.is_equal).then_inc(hit_ready, 1)
                past(dve, hit_ready, n)
                nc.vector.tensor_tensor(e_w2[b][:, :, :], e_hit[b][:, :, :], xe[b][:, :, COL_W:COL_W + 2], ALU.mult).then_inc(wsel_ready, 1)
                past(dve, wsel_ready, n)
                past(dve, y_scaled, n, 2, CB)
                nc.vector.tensor_reduce(e_w[b][:, :], e_w2[b][:, :, :], AX_X, ALU.add).then_inc(wts_ready, 1)
                past(dve, y_added[b], e * (NCH // 2) + c // 2, 1, 16 * CB)
                nc.vector.tensor_copy(e_tok[b][:, :], xe[b][:, :, COL_TOK]).then_inc(toks_ready, 1)
                dve.wait_ge(xe_transposed, n * 2 + 2)
                past(dve, h_done, n, 2, 3)
                nc.vector.tensor_copy(xeT[b][:, 1, :], p2_xT[1][:, :, :].rearrange("p b q -> p (b q)")).then_inc(xeT_vector, 1)
                for j in range(FF // P):
                    m = n * 3 + j
                    past(dve, silu_done, m)
                    if j == 0:
                        past(dve, y_done, n, 2, 2)
                    q = (c * 3 + j) % 2
                    nc.vector.tensor_tensor(hT[b][:, j, :], silu[q][:, :], p2_h[q][1][:, :, :].rearrange("p b q -> p (b q)"),
                                            ALU.mult).then_inc(h_ready, 1)

            def next_expert(e):
                dve.wait_ge(hit_ready, (e + 1) * NCH)
                nc.vector.tensor_scalar(e_now[:, :], e_now[:, :], 1.0, None, ALU.add).then_inc(e_number, 1)
                dve.wait_ge(e_number, e + 2)

            for c in range(NCH):
                chunk(0, c)
            next_expert(0)
            with dve.Fori(1, NEXP) as e:
                for c in range(NCH):
                    chunk(e, c)
                next_expert(e)


_INS = ['L0_attn_x', 'L0_attn_Wq', 'L0_attn_Wk', 'L0_attn_Wv', 'L0_attn_Wo', 'L0_attn_lambda_q1', 'L0_attn_lambda_k1',
        'L0_attn_lambda_q2', 'L0_attn_lambda_k2', 'L0_attn_ln_w', 'L0_attn_ln_b', 'L0_ffn_w_gate', 'L0_ffn_c_fc',
        'L0_ffn_c_proj']


def kernel(**inputs):
    import numpy as _np
    import concourse.bacc as _bacc
    from concourse import mybir as _mybir
    from concourse.bass_utils import run_bass_kernel_spmd as _run

    nc = _bacc.Bacc("TRN2", target_bir_lowering=False, num_devices=1)
    arrays, args = {}, []
    for name in _INS:
        a = _np.ascontiguousarray(inputs[name])
        arrays[f"in_{name}_dram"] = a
        args.append(nc.dram_tensor(f"in_{name}_dram", a.shape, _mybir.dt.from_np(a.dtype), kind="ExternalInput").ap())
    b, s, e = inputs["L0_attn_x"].shape
    args.append(nc.dram_tensor("out_0_dram", (b * s + CAP, e), _mybir.dt.float32, kind="ExternalOutput").ap())
    build_block(nc, *args)
    r = _run(nc, [arrays], core_ids=[0])
    return r.results[0]["out_0_dram"][:b * s].reshape(b, s, e)
```

```python
import math

import concourse.bass as bass
from concourse import mybir
from contextlib import ExitStack

P = 128
E = 256
H = 8
D = 16
DV = 2 * D
CAP = 1024
NEXP = 8
FF = 384
FOLD = 2
EPS_LN = 1e-5
EPS_RMS = 1e-8
LAMBDA_INIT = 0.8 - 0.6 * math.exp(-0.3 * 12)
SCORE_SCALE = 1.0 / D ** 0.25
COL_EXP, COL_W, COL_TOK, ROW = E, E + 2, E + 4, E + 8
OUT_OF_TABLE = float(1 << 20)
LN_EXP_SET = 6
GROUP = 4
UNROLL = 8
TURN = 16
RMS_SCALE = math.sqrt(EPS_LN / (EPS_RMS * DV))

F32 = mybir.dt.float32
F32R = mybir.dt.float32r
BF16 = mybir.dt.bfloat16
I32 = mybir.dt.int32
U32 = mybir.dt.uint32
ALU = mybir.AluOpType
ACT = mybir.ActivationFunctionType
AX_X = mybir.AxisListType.X


def build_block(nc, x, wq, wk, wv, wo, lq1, lk1, lq2, lk2, ln_w, ln_b, w_gate, c_fc, c_proj, out):
    NTOK = x.shape[0] * x.shape[1]
    NT = NTOK // P
    NBLK = CAP // P
    CB = 4
    NCH = NBLK // CB
    SLOTS = NEXP * CAP
    x_rows = x.rearrange("b s e -> (b s) e")
    table = nc.dram_tensor("slot_table", [SLOTS, ROW], F32, kind="Internal").ap()

    with ExitStack() as ctx:
        def sb(name, shape, dt=F32):
            return ctx.enter_context(nc.sbuf_tensor(name, shape, dt))

        def pb(name, shape, dt=F32):
            return ctx.enter_context(nc.psum_tensor(name, shape, dt))

        def sem(name):
            return ctx.enter_context(nc.semaphore(name))

        wqkv = sb("wqkv", [P, 2, 3 * E])
        wo_sb = sb("wo_sb", [P, 2, E])
        wg_sb = sb("wg_sb", [P, 2, NEXP])
        ident = sb("ident", [P, P])
        tri = sb("tri", [P, P], BF16)
        ones = sb("ones", [P, P], BF16)
        ebase = sb("ebase", [1, NEXP], BF16)
        elimit = sb("elimit", [P, NEXP])
        eiota = sb("eiota", [P, NEXP])
        tok_all = sb("tok_all", [P, NT])
        lam_in = sb("lam_in", [P, 2, 2, D])
        lam_prod = sb("lam_prod", [P, 2, D])
        lam_sum = sb("lam_sum", [P, 2])
        lam_exp = sb("lam_exp", [P, 2])
        neg_lam = sb("neg_lam", [P, 1])
        lnwb = sb("lnwb", [P, 2])
        lnwb_s = sb("lnwb_s", [P, 2])
        eps_ln = sb("eps_ln", [P, 1])
        fill = sb("fill", [P, NBLK, ROW])
        two = range(2)

        def pair(name, shape, dt=F32):
            return [sb(f"{name}{b}", shape, dt) for b in two] * (UNROLL // 2)

        stat = pair("stat", [P, H + 2, 2])
        stat_ln = pair("stat_ln", [P, H + 2])
        rstd = pair("rstd", [P, H + 2])
        neg_mr = pair("neg_mr", [P, 2])
        bn1, bn2 = pair("bn1", [P, 6]), pair("bn2", [P, 6])
        xn = pair("xn", [P, E])
        xT = pair("xT", [P, 2, P])
        k_sb, v_sb = pair("k_sb", [P, E]), pair("v_sb", [P, E])
        qk_prod = sb("qk_prod", [P, H * H * 2 * D])
        s_raw = pair("s_raw", [P, H, H, 2])
        s_max = pair("s_max", [P, H, 2])
        s_sub = pair("s_sub", [P, 2, H, H])
        probs = pair("probs", [P, 2, H, H])
        p_sum, p_rec = pair("p_sum", [P, 2 * H]), pair("p_rec", [P, 2 * H])
        p_norm = pair("p_norm", [P, 2, H, H])
        w_att = pair("w_att", [P, H, H])
        v_prod = pair("v_prod", [P, H, H, DV])
        a_sb = pair("a_sb", [P, E])
        a_sq = pair("a_sq", [P, H, DV])
        a_n = pair("a_n", [P, E])
        aT = pair("aT", [P, 2, P])
        rows = sb("rows", [P, UNROLL, ROW])
        x2T = pair("x2T", [P, 2, P])
        g_max = pair("g_max", [P, GROUP])
        g_sub, g_exp = pair("g_sub", [P, GROUP, NEXP]), pair("g_exp", [P, GROUP, NEXP])
        g_sum, g_rec = pair("g_sum", [P, GROUP]), pair("g_rec", [P, GROUP])
        g_top, g_idx = pair("g_top", [P, GROUP, 8]), pair("g_idx", [P, GROUP, 8], U32)
        g_hot = pair("g_hot", [P, GROUP, 2, NEXP])
        g_mask = pair("g_mask", [P, GROUP, NEXP], BF16)
        g_count = pair("g_count", [P, NEXP])
        g_before = pair("g_before", [P, NEXP], BF16)
        g_over, g_slot8 = pair("g_over", [P, GROUP, NEXP]), pair("g_slot8", [P, GROUP, NEXP])
        g_sel = pair("g_sel", [P, GROUP, 2, NEXP])
        g_slotf, g_slot = pair("g_slotf", [P, GROUP, 2]), pair("g_slot", [P, GROUP, 2], I32)
        NHT = FF // P
        w1 = [sb(f"w1{b}", [P, 2, 2 * FF]) for b in two]
        w2 = [sb(f"w2{b}", [P, NHT, E]) for b in two]
        w1_hi, w1_lo = ([sb(f"w1_{part}{b}", [P, 2, 2 * FF], F32R) for b in two] for part in ("hi", "lo"))
        w2_hi, w2_lo = ([sb(f"w2_{part}{b}", [P, NHT, E], F32R) for b in two] for part in ("hi", "lo"))
        xe = [sb(f"xe{b}", [P, CB, ROW]) for b in two]
        e_hit = [sb(f"e_hit{b}", [P, CB, 2]) for b in two]
        e_w2 = [sb(f"e_w2{b}", [P, CB, 2]) for b in two]
        e_w = [sb(f"e_w{b}", [P, CB]) for b in two]
        e_tok = [sb(f"e_tok{b}", [P, CB], I32) for b in two]

        with nc.sbuf_tensor("x_all", [P, NT, E], F32) as x_all:
            pass
        x_hi, x_lo = ([sb(f"x_{part}{b}", [P, 2, CB * P], F32R) for b in two] for part in ("hi", "lo"))
        h_hi, h_lo = ([sb(f"h_{part}{b}", [P, NHT, CB * P], F32R) for b in two] for part in ("hi", "lo"))
        silu = [sb(f"silu{b}", [P, CB * P]) for b in two]
        hidden = [sb(f"hidden{b}", [P, CB * P]) for b in two]
        y_sb = [sb(f"y_sb{b}", [P, CB, E]) for b in two]

        bank_t = pb("bank_t", [P, 4, P])
        bank_t2 = pb("bank_t2", [P, 4, P])
        bank_qk = [pb(f"bank_qk{b}", [P, 2, E]) for b in two] * (UNROLL // 2)
        bank_v = pb("bank_v", [P, 2, E])
        bank_a = pb("bank_a", [P, 2, E])
        bank_wo = pb("bank_wo", [P, 2, E])
        bank_g = pb("bank_g", [P, 2, E])
        logits = bank_g[:, 0, 0:GROUP * NEXP].rearrange("p (j e) -> p j e", e=NEXP)
        slots_ps = bank_g[:, 1, 0:GROUP * NEXP].rearrange("p (j e) -> p j e", e=NEXP)
        p2_xT = [bank_t, bank_t2]
        p2_h = [[bank_qk[0], bank_qk[1]], [bank_v, bank_a]]
        p2_y = [bank_wo, bank_g]

        x_loaded = [sem(f"x_loaded{c}") for c in range(4)]
        wqkv_loaded, w_loaded = sem("wqkv_loaded"), sem("w_loaded")
        consts = sem("consts")
        pool_chain = sem("pool_chain")
        lam_chain = sem("lam_chain")
        lam_ready = sem("lam_ready")
        filled = sem("filled")
        ln1_stats, ln1_aggr, ln2_stats, ln2_aggr, stat_log, rstd_ready, neg_mr_ready, xn_ready, xn2_ready = (
            sem(n) for n in "ln1_stats ln1_aggr ln2_stats ln2_aggr stat_log rstd_ready neg_mr_ready xn_ready xn2_ready".split())
        xn_transposed, xT_copied, qkv_done, k_copied, v_copied, qk_multiplied = (
            sem(n) for n in "xn_transposed xT_copied qkv_done k_copied v_copied qk_multiplied".split())
        scores_ready, smax_ready, ssub_ready, exp_done, psum_ready, prec_ready, pnorm_ready, w_ready, multiplied, products_ready = (
            sem(n) for n in "scores_ready smax_ready ssub_ready exp_done psum_ready prec_ready pnorm_ready w_ready multiplied products_ready".split())
        a_summed, a_copied, ms_ready, an_ready, an_transposed, aT_copied, wo_done, x1_ready = (
            sem(n) for n in "a_summed a_copied ms_ready an_ready an_transposed aT_copied wo_done x1_ready".split())
        xn2_transposed, x2T_copied, logits_ready = (
            sem(n) for n in "xn2_transposed x2T_copied logits_ready".split())
        gmax_ready, gsub_ready, gexp_done, gsum_ready, gtop_ready, grec_ready, gidx_ready = (
            sem(n) for n in "gmax_ready gsub_ready gexp_done gsum_ready gtop_ready grec_ready gidx_ready".split())
        gweights_ready, gexperts_ready, gtokens_ready, ghot_ready, gmask_ready, gcount_ready, before_ready, pos_ready = (
            sem(n) for n in "gweights_ready gexperts_ready gtokens_ready ghot_ready gmask_ready gcount_ready before_ready pos_ready".split())
        over_ready, slot8_ready, sel_ready, slotf_ready, slot_ready = (
            sem(n) for n in "over_ready slot8_ready sel_ready slotf_ready slot_ready".split())
        scattered = [sem(f"scattered{r}") for r in range(UNROLL)]
        x1_stored = sem("x1_stored")
        e_loaded = [sem(f"e_loaded{b}") for b in two]
        xe_loaded = [sem(f"xe_loaded{b}") for b in two]
        w_hi_ready, w_lo_ready = sem("w_hi_ready"), sem("w_lo_ready")
        hit_ready, wsel_ready, wts_ready, toks_ready = sem("hit_ready"), sem("wsel_ready"), sem("wts_ready"), sem("toks_ready")
        xe_transposed, x_hi_ready, x_lo_ready = (
            sem(n) for n in "xe_transposed x_hi_ready x_lo_ready".split())
        h_done, silu_done, gated, h_hi_ready, h_lo_ready = (
            sem(n) for n in "h_done silu_done gated h_hi_ready h_lo_ready".split())
        y_done = sem("y_done")
        y_scaled = sem("y_scaled")
        y_added = [sem(f"y_added{b}") for b in two]

        def past(eng, s, t, back=0, per=1):
            if isinstance(t, int):
                if t - back < 0:
                    return
            eng.wait_ge(s, (t - (back - 1)) * per)

        LAG_MAX = 13
        FIRST = 2 * UNROLL

        def row_free(eng, t, r):
            if isinstance(t, int) and t < UNROLL:
                return
            eng.wait_ge(scattered[r], (t - r) * (32 // UNROLL))

        def run_tiles(eng, step):
            for i in range(FIRST):
                step(i, i % UNROLL, i // GROUP)
            with eng.Fori(0, (NT - FIRST) // TURN) as turn:
                for v in range(TURN):
                    step(turn * TURN + (FIRST + v), v % UNROLL, turn * (TURN // GROUP) + (FIRST + v) // GROUP)
            for i in range(NT, NT + LAG_MAX):
                step(i, i % UNROLL, i // GROUP)

        def live(i, lag):
            return not isinstance(i, int) or 0 <= i - lag < NT

        CHUNKS = NEXP * NCH

        def run_chunks(eng, step):
            turn_steps = 2 * NCH
            for m in range(turn_steps):
                step(m, m % turn_steps, m // turn_steps)
            with eng.Fori(1, CHUNKS // turn_steps) as turn:
                for v in range(turn_steps):
                    step(turn * turn_steps + v, v, turn)
            for m in range(CHUNKS, CHUNKS + 2):
                step(m, m % turn_steps, m // turn_steps)

        def chunk_live(m, lag):
            return not isinstance(m, int) or 0 <= m - lag < CHUNKS

        def second_layer_after(m):
            return NHT - 1 if isinstance(m, int) and m == CHUNKS else 0

        def expert_of(v, turn, lag):
            return turn * 2 + (v - lag) // NCH

        def roots_live(i):
            return not isinstance(i, int) or i < NT + 7

        def group_live(q):
            return not isinstance(q, int) or 0 <= q - 3 < NT // GROUP

        def upto(eng, s, t, back=0):
            past(eng, s, min(t, NT - 1) if isinstance(t, int) else t, back)

        def x_tile(t):
            if isinstance(t, int):
                return x_all[:, t, :]
            return x_all[:, bass.ds(t, 1), :].rearrange("p a e -> p (a e)")

        W_LOADS = 16 * (4 + 2 * (P // DV) + 2)

        block = ctx.enter_context(nc.Block())

        @block.sync
        def _(sp):
            xv = x_rows.rearrange("(t p) e -> p t e", p=P)
            parts = [(0, 2), (2, 6), (6, 14), (14, NT)]
            sp.dma_start(x_all[:, 0:2, :], xv[:, 0:2, :]).then_inc(x_loaded[0], 16)
            for j, w in enumerate((wq, wk, wv)):
                sp.dma_start(wqkv[:, :, j * E:(j + 1) * E], w.rearrange("(k p) n -> p k n", p=P)).then_inc(wqkv_loaded, 16)
            sp.dma_start(x_all[:, 2:6, :], xv[:, 2:6, :]).then_inc(x_loaded[1], 16)
            for i, v in enumerate((lq1, lk1, lq2, lk2)):
                sp.dma_start(lam_in[:, i // 2, i % 2, :], v.rearrange("(a d) -> a d", a=1).to_broadcast([P, D])).then_inc(w_loaded, 16)
            sp.dma_start(wo_sb[:, :, :], wo.rearrange("(k p) n -> p k n", p=P)).then_inc(w_loaded, 16)
            sp.dma_start(wg_sb[:, :, :], w_gate.rearrange("(k p) n -> p k n", p=P)).then_inc(w_loaded, 16)
            for r in range(P // DV):
                for c, v in enumerate((ln_w, ln_b)):
                    sp.dma_start(lnwb[r * DV:(r + 1) * DV, c:c + 1], v.rearrange("(d a) -> d a", a=1)).then_inc(w_loaded, 16)
            sp.wait_ge(w_loaded, W_LOADS)
            for c in range(2, 4):
                a, b = parts[c]
                sp.dma_start(x_all[:, a:b, :], xv[:, a:b, :]).then_inc(x_loaded[c], 16)
            sp.wait_ge(consts, 2)
            for e in range(NEXP):
                sp.dma_start(table[e * CAP:(e + 1) * CAP, :].rearrange("(b p) w -> p b w", p=P), fill[:, :, :]).then_inc(filled, 16)
            sp.dma_start(out[NTOK:NTOK + CAP, :].rearrange("(b p) w -> p b w", p=P), fill[:, :, 0:E]).then_inc(filled, 16)
            for e in range(2):
                sp.dma_start(w1[e][:, :, :], c_fc[e].rearrange("(k p) f -> p k f", p=P)).then_inc(e_loaded[e], 16)
                sp.dma_start(w2[e][:, :, :], c_proj[e].rearrange("(k p) n -> p k n", p=P)).then_inc(e_loaded[e], 16)
            ov = out[0:NTOK, :].rearrange("(t p) e -> p t e", p=P)
            for c in range(NT // 8):
                sp.wait_ge(x1_ready, 8 * (c + 1))
                sp.dma_start(ov[:, 8 * c:8 * c + 8, :], x_all[:, 8 * c:8 * c + 8, :]).then_inc(x1_stored, 16)
            for r in range(UNROLL):
                sp.wait_ge(scattered[r], 32 * NT // UNROLL)
            sp.wait_ge(filled, 16 * (NEXP + 1))

            def load_chunk(n, b):
                past(sp, xe_transposed, n, 2, 2)
                past(sp, hit_ready, n, 2)
                past(sp, wsel_ready, n, 2)
                past(sp, toks_ready, n, 2)
                src = table.rearrange("(n b p) w -> n p b w", b=CB, p=P)
                s = src[n] if isinstance(n, int) else src[bass.ds(n, 1)].rearrange("n p b w -> (n p) b w")
                sp.dma_start(xe[b][:, :, :], s).then_inc(xe_loaded[b], 16)

            def load_expert(e, b):
                past(sp, w_hi_ready, e, 2, 2)
                past(sp, w_lo_ready, e, 2, 2)
                s1 = c_fc[bass.ds(e, 1)].rearrange("a (k p) f -> p (a k) f", p=P)
                s2 = c_proj[bass.ds(e, 1)].rearrange("a (k p) f -> p (a k) f", p=P)
                sp.dma_start(w1[b][:, :, :], s1).then_inc(e_loaded[b], 16)
                sp.dma_start(w2[b][:, :, :], s2).then_inc(e_loaded[b], 16)

            for n in range(2 * NCH):
                load_chunk(n, n % 2)
            with sp.Fori(1, NEXP // 2) as h:
                for u in range(2):
                    load_expert(h * 2 + u, u)
                    for c in range(NCH):
                        load_chunk(h * (2 * NCH) + (u * NCH + c), (u * NCH + c) % 2)

        @block.gpsimd
        def _(pool):
            n = 0

            def chain(ins):
                nonlocal n
                ins.then_inc(pool_chain, 1)
                n += 1

            chain(pool.memset(ident[:, :], 0.0))
            pool.wait_ge(pool_chain, n)
            chain(pool.affine_select(out=ident[:, :], in_=ident[:, :], compare_op=ALU.not_equal, fill=1.0, base=0,
                                     pattern=[[-1, P]], channel_multiplier=1))
            chain(pool.memset(eps_ln[:, :], EPS_LN))
            for b in two:
                chain(pool.memset(stat[b][:, :, :], 1.0))
            pool.wait_ge(pool_chain, n)
            pool.nop().then_inc(consts, 1)
            chain(pool.memset(ones[:, :], 1.0))
            pool.wait_ge(pool_chain, n)
            chain(pool.affine_select(out=tri[:, :], in_=ones[:, :], compare_op=ALU.is_gt, fill=0.0, base=0,
                                     pattern=[[1, P]], channel_multiplier=-1))
            for i, (t, step, base) in enumerate(((eiota, 1, 0), (elimit, CAP, CAP))):
                chain(pool.iota(t[:, :], pattern=[[step, NEXP]], base=base, channel_multiplier=0,
                                allow_small_or_imprecise_dtypes=True))
            chain(pool.iota(ebase[:, :], pattern=[[CAP, NEXP]], base=0, channel_multiplier=0,
                            allow_small_or_imprecise_dtypes=True))
            chain(pool.iota(tok_all[:, :], pattern=[[P, NT]], base=0, channel_multiplier=1,
                            allow_small_or_imprecise_dtypes=True))
            chain(pool.memset(g_before[0][:, :], 0.0))
            chain(pool.memset(rows[:, :, :], 0.0))
            chain(pool.memset(fill[:, :, :], 0.0))
            pool.wait_ge(pool_chain, n)
            chain(pool.iota(fill[:, :, COL_TOK], pattern=[[P, NBLK]], base=NTOK, channel_multiplier=1,
                            allow_small_or_imprecise_dtypes=True))
            pool.wait_ge(pool_chain, n)
            pool.nop().then_inc(consts, 1)

            def products(t, b):
                past(pool, w_ready, t)
                past(pool, v_copied, t)
                past(pool, a_summed, t, 2)
                pool.tensor_tensor(
                    v_prod[b][:, :, :, :],
                    w_att[b][:, :, :].rearrange("p n m -> p m n").unsqueeze(3).to_broadcast([P, H, H, DV]),
                    v_sb[b][:, :].rearrange("p (m e) -> p m e", m=H).unsqueeze(2).to_broadcast([P, H, H, DV]),
                    ALU.mult).then_inc(multiplied, 1)
                past(pool, multiplied, t)
                pool.tensor_tensor(v_prod[b][:, 0:FOLD, :, :].rearrange("p m n e -> p (m n e)"),
                                   v_prod[b][:, 0:FOLD, :, :].rearrange("p m n e -> p (m n e)"),
                                   v_prod[b][:, H - FOLD:, :, :].rearrange("p m n e -> p (m n e)"),
                                   ALU.add).then_inc(products_ready, 1)

            def rms_scale(t, b, u):
                past(pool, rstd_ready, t, -5)
                past(pool, a_copied, t)
                past(pool, an_transposed, t, 2)
                pool.tensor_tensor(a_n[b][:, :].rearrange("p (n e) -> p n e", n=H),
                                   a_sb[b][:, :].rearrange("p (n e) -> p n e", n=H),
                                   rstd[u][:, 0:H].unsqueeze(2).to_broadcast([P, H, DV]),
                                   ALU.mult).then_inc(an_ready, 1)

            def row_waits(g):
                past(pool, slot_ready, g)
                past(pool, gweights_ready, g)
                past(pool, gexperts_ready, g)
                past(pool, gtokens_ready, g)
                if isinstance(g, int) and g == 0:
                    pool.wait_ge(filled, 16 * (NEXP + 1))

            def scatter(t, r):
                gb, j = r // GROUP, r % GROUP
                for k in range(2):
                    pool.indirect_dma_start(
                        out=table, out_offset=bass.IndirectOffsetOnAxis(ap=g_slot[gb][:, j, k:k + 1], axis=0),
                        in_=rows[:, r, :], in_offset=None, bounds_check=SLOTS - 1, oob_is_err=False,
                    ).then_inc(scattered[r], 16)

            def step(i, u, q):
                if live(i, 5):
                    rms_scale(i - 5, (u - 5) % UNROLL, u)
                if live(i, 13):
                    past(pool, xn2_ready, i - 13)
                    if u % GROUP == 1:
                        row_waits(q - 3)
                if live(i, 3):
                    products(i - 3, (u - 3) % UNROLL)
                if live(i, 13):
                    scatter(i - 13, (u - 13) % UNROLL)

            run_tiles(pool, step)

            pool.wait_ge(x1_stored, 16 * (NT // 8))

            def weights_low(e):
                for k, (w, hi, lo) in enumerate(((w1, w1_hi, w1_lo), (w2, w2_hi, w2_lo))):
                    b = e % 2
                    pool.wait_ge(e_loaded[b], (e // 2 + 1) * 32)
                    past(pool, w_hi_ready, 2 * e + k)
                    past(pool, (h_done, y_done)[k], e, 2, NCH * (NHT, 2)[k])
                    pool.tensor_tensor(lo[b][:, :, :].rearrange("p k n -> p (k n)"), w[b][:, :, :].rearrange("p k n -> p (k n)"),
                                       hi[b][:, :, :].rearrange("p k n -> p (k n)"), ALU.subtract).then_inc(w_lo_ready, 1)

            def add_chunk(n):
                past(pool, toks_ready, n)
                if n % NCH == 0:
                    for b in two:
                        if n > 0:
                            pool.wait_ge(y_added[b], 16 * CB * (NCH // 2) * (n // NCH))
                for k in range(CB):
                    pool.wait_ge(y_scaled, n * CB + k + 1)
                    pool.indirect_dma_start(
                        out=out, out_offset=bass.IndirectOffsetOnAxis(ap=e_tok[n % 2][:, k:k + 1], axis=0),
                        in_=y_sb[n % 2][:, k, :], in_offset=None, compute_op=ALU.add,
                    ).then_inc(y_added[n % 2], 16)

            for m in range(CHUNKS + 2):
                if m % NCH == 0 and m < CHUNKS:
                    weights_low(m // NCH)
                if chunk_live(m, 2):
                    add_chunk(m - 2)
            for b in two:
                pool.wait_ge(y_added[b], 16 * CB * (NCH // 2) * NEXP)

        @block.scalar
        def _(act):
            act.add_instruction(mybir.InstLoadActFuncSet(name=nc.get_next_instruction_name(), ins=[], outs=[], act_func_set_id=LN_EXP_SET))
            act.wait_ge(consts, 1)

            def lambda_exps():
                act.wait_ge(lam_chain, 2)
                act.wait_ge(consts, 2)
                nc.scalar.activation(lam_exp[:, :], lam_sum[:, :], ACT.Exp).then_inc(lam_ready, 1)

            def copy_xT(t, b):
                past(act, xn_transposed, t)
                past(act, qkv_done, t, 2)
                nc.scalar.copy(xT[b][:, :, :], bank_t[:, 0:2, :]).then_inc(xT_copied, 1)

            def copy_kv(t, b):
                past(act, qkv_done, t)
                past(act, qk_multiplied, t, 2)
                nc.scalar.copy(k_sb[b][:, :], bank_qk[b][:, 1, :]).then_inc(k_copied, 1)
                past(act, products_ready, t, 2)
                nc.scalar.copy(v_sb[b][:, :], bank_v[:, 0, :]).then_inc(v_copied, 1)

            def exp_scores(t, b):
                past(act, ssub_ready, t)
                past(act, pnorm_ready, t, 2)
                nc.scalar.activation(probs[b][:, :, :, :], s_sub[b][:, :, :, :], ACT.Exp, scale=SCORE_SCALE).then_inc(exp_done, 1)

            def copy_a(t, b):
                past(act, a_summed, t)
                past(act, an_ready, t, 2)
                nc.scalar.copy(a_sb[b][:, :], bank_a[:, 0, :]).then_inc(a_copied, 1)

            def square(t, b, u):
                past(act, a_copied, t)
                for h in range(H):
                    last = nc.scalar.activation(a_sq[b][:, h, :], a_sb[b][:, h * DV:(h + 1) * DV], ACT.Square,
                                                scale=RMS_SCALE, accum_out=stat[u][:, h, 1:2])
                last.then_inc(ms_ready, 1)

            def copy_aT(t, b):
                if isinstance(t, int) and t == 0:
                    act.wait_ge(lam_ready, 3)
                past(act, an_transposed, t)
                if live(t + 6, 8):
                    upto(act, xn2_transposed, t, 2)
                past(act, wo_done, t, 2)
                nc.scalar.activation(aT[b][:, :, :], bank_t2[:, 2:4, :], ACT.Identity, bias=lnwb_s[:, 1:2],
                                     scale=lnwb_s[:, 0:1]).then_inc(aT_copied, 1)

            def copy_x2T(t, b):
                past(act, xn2_transposed, t)
                past(act, logits_ready, t, 2)
                nc.scalar.copy(x2T[b][:, :, :], bank_t2[:, 0:2, :]).then_inc(x2T_copied, 1)

            def exp_gate(g, gb):
                past(act, gsub_ready, g)
                past(act, gidx_ready, g, 2)
                past(act, gsum_ready, g, 2)
                nc.scalar.activation(g_exp[gb][:, :, :], g_sub[gb][:, :, :], ACT.Exp).then_inc(gexp_done, 1)

            def roots(i, u):
                if live(i, 1):
                    past(act, ln1_aggr, i - 1)
                if live(i, 5):
                    past(act, ms_ready, i - 5)
                if live(i, 7):
                    past(act, ln2_aggr, i - 7)
                nc.scalar.activation(stat_ln[u][:, :], stat[u][:, :, 1], ACT.Ln, bias=eps_ln[:, :]).then_inc(stat_log, 1)
                past(act, stat_log, i)
                past(act, neg_mr_ready, i, 2)
                if live(i, 7):
                    past(act, an_ready, i - 7)
                nc.scalar.activation(rstd[u][:, :], stat_ln[u][:, :], ACT.Exp, scale=-0.5).then_inc(rstd_ready, 1)

            def normalise_waits(i, u):
                past(act, neg_mr_ready, i)
                if live(i, 1):
                    past(act, xn_transposed, i - 1, 2)
                if live(i, 7):
                    row_free(act, i - 7, (u - 7) % UNROLL)

            def normalise1(t, u):
                nc.scalar.activation(xn[(u - 1) % UNROLL][:, :], x_tile(t), ACT.Identity, bias=neg_mr[u][:, 0:1],
                                     scale=rstd[u][:, H:H + 1]).then_inc(xn_ready, 1)

            def normalise2(t, u, r):
                nc.scalar.activation(rows[:, r, 0:E], x_tile(t), ACT.Identity, bias=neg_mr[u][:, 1:2],
                                     scale=rstd[u][:, H + 1:H + 2]).then_inc(xn2_ready, 1)

            def step(i, u, q):
                if isinstance(i, int) and i == 2:
                    lambda_exps()
                if live(i, 5):
                    copy_a(i - 5, (u - 5) % UNROLL)
                if live(i, 6):
                    copy_aT(i - 6, (u - 6) % UNROLL)
                if live(i, 8):
                    copy_x2T(i - 8, (u - 8) % UNROLL)
                if u % GROUP == 0 and group_live(q):
                    exp_gate(q - 3, (u // GROUP - 3) % 2)
                if live(i, 5):
                    square(i - 5, (u - 5) % UNROLL, u)
                if roots_live(i):
                    roots(i, u)
                if live(i, 2):
                    copy_kv(i - 2, (u - 2) % UNROLL)
                if roots_live(i):
                    normalise_waits(i, u)
                if live(i, 3):
                    exp_scores(i - 3, (u - 3) % UNROLL)
                if live(i, 1):
                    normalise1(i - 1, u)
                if live(i, 7):
                    normalise2(i - 7, u, (u - 7) % UNROLL)
                if live(i, 1):
                    copy_xT(i - 1, (u - 1) % UNROLL)

            run_tiles(act, step)

            def weights_high(e, b):
                act.wait_ge(e_loaded[b], e * 16 + (2 - b) * 16)
                past(act, h_done, e, 2, NCH * NHT)
                past(act, w_lo_ready, e, 2, 2)
                nc.scalar.copy(w1_hi[b][:, :, :], w1[b][:, :, :]).then_inc(w_hi_ready, 1)
                past(act, y_done, e, 2, NCH * 2)
                nc.scalar.copy(w2_hi[b][:, :, :], w2[b][:, :, :]).then_inc(w_hi_ready, 1)

            def input_high(n, b):
                past(act, h_done, n, 2, NHT)
                past(act, x_lo_ready, n, 2, 2)
                for k in range(2):
                    act.wait_ge(xe_transposed, n * 2 + k + 1)
                    nc.scalar.copy(x_hi[b][:, k, :], p2_xT[k][:, :, :].rearrange("p b q -> p (b q)")).then_inc(x_hi_ready, 1)

            def silu_of(n, j, q):
                act.wait_ge(h_done, n * NHT + j + 1)
                past(act, gated, n * NHT + j, 2)
                nc.scalar.activation(silu[q][:, :], p2_h[q][0][:, :, :].rearrange("p b q -> p (b q)"),
                                     ACT.Silu).then_inc(silu_done, 1)

            def hidden_high(n, b, j, q):
                if j == 0:
                    past(act, y_done, n, 2, 2)
                    past(act, h_lo_ready, n, 2, NHT)
                act.wait_ge(gated, n * NHT + j + 1)
                nc.scalar.copy(h_hi[b][:, j, :], hidden[q][:, :]).then_inc(h_hi_ready, 1)

            def scale_output(n, b):
                act.wait_ge(wts_ready, n + 1)
                if not isinstance(n, int) or n >= 2:
                    act.wait_ge(y_added[b], (n - b) * (8 * CB))
                for k in range(CB):
                    act.wait_ge(y_done, n * 2 + k // 2 + 1)
                    nc.scalar.activation(y_sb[b][:, k, :], p2_y[k // 2][:, k % 2, :], ACT.Copy, scale=e_w[b][:, k:k + 1]).then_inc(y_scaled, 1)

            def chunk_step(m, v, turn):
                if v % NCH == 0 and chunk_live(m, 0):
                    weights_high(expert_of(v, turn, 0), (v // NCH) % 2)
                b0, b1, b2 = v % 2, (v - 1) % 2, (v - 2) % 2
                tiles = [(j, (b1 * NHT + j) % 2) for j in range(NHT)]
                for j, q in tiles:
                    if chunk_live(m, 1):
                        silu_of(m - 1, j, q)
                    if j == 0 and chunk_live(m, 0):
                        input_high(m, b0)
                    if chunk_live(m, 1):
                        hidden_high(m - 1, b1, j, q)
                    if j == second_layer_after(m) and chunk_live(m, 2):
                        scale_output(m - 2, b2)

            act.wait_ge(x1_stored, 16 * (NT // 8))
            run_chunks(act, chunk_step)

        @block.tensor
        def _(pe):
            pe.wait_ge(consts, 1)

            def transpose_x(t, b):
                past(pe, xn_ready, t)
                past(pe, xT_copied, t, 1)
                for k in range(2):
                    last = nc.tensor.transpose(bank_t[:, k, :], xn[b][:, k * P:(k + 1) * P], ident[:, :])
                last.then_inc(xn_transposed, 1)

            def project(t, b):
                if isinstance(t, int) and t == 0:
                    pe.wait_ge(wqkv_loaded, 16 * 3)
                    pe.wait_ge(consts, 2)
                past(pe, xT_copied, t)
                past(pe, qk_multiplied, t, 2)
                for k in range(2):
                    nc.tensor.matmul(bank_qk[b][:, :, :].rearrange("p a e -> p (a e)"), xT[b][:, k, :],
                                     wqkv[:, k, 0:2 * E], start=(k == 0), stop=(k == 1))
                past(pe, v_copied, t, 1)
                for k in range(2):
                    last = nc.tensor.matmul(bank_v[:, 0, :], xT[b][:, k, :], wqkv[:, k, 2 * E:3 * E],
                                            start=(k == 0), stop=(k == 1))
                last.then_inc(qkv_done, 1)

            def sum_heads(t, b):
                past(pe, products_ready, t)
                past(pe, a_copied, t, 1)
                for m in range(H - FOLD):
                    last = nc.tensor.matmul(bank_a[:, 0, :], ident[:, :],
                                            v_prod[b][:, m, :, :].rearrange("p n e -> p (n e)"),
                                            start=(m == 0), stop=(m == H - FOLD - 1))
                last.then_inc(a_summed, 1)

            def transpose_a(t, b):
                past(pe, an_ready, t)
                past(pe, aT_copied, t, 1)
                past(pe, x2T_copied, t, 3)
                for k in range(2):
                    last = nc.tensor.transpose(bank_t2[:, 2 + k, :], a_n[b][:, k * P:(k + 1) * P], ident[:, :])
                last.then_inc(an_transposed, 1)

            def out_project(t, b):
                if isinstance(t, int) and t == 0:
                    pe.wait_ge(w_loaded, W_LOADS)
                past(pe, aT_copied, t)
                past(pe, x1_ready, t, 1)
                for k in range(2):
                    last = nc.tensor.matmul(bank_wo[:, 0, :], aT[b][:, k, :], wo_sb[:, k, :], start=(k == 0), stop=(k == 1))
                last.then_inc(wo_done, 1)

            def transpose_x2(t, r):
                past(pe, xn2_ready, t)
                past(pe, x2T_copied, t, 1)
                upto(pe, aT_copied, t + 1)
                for k in range(2):
                    last = nc.tensor.transpose(bank_t2[:, k, :], rows[:, r, k * P:(k + 1) * P], ident[:, :])
                last.then_inc(xn2_transposed, 1)

            def gate(t, r, q):
                past(pe, x2T_copied, t)
                j = r % GROUP
                if j == 0:
                    past(pe, gsub_ready, q - 3)
                if j == 1:
                    past(pe, slot8_ready, q - 3)
                for k in range(2):
                    last = nc.tensor.matmul(logits[:, j, :], x2T[r][:, k, :], wg_sb[:, k, :], start=(k == 0), stop=(k == 1))
                last.then_inc(logits_ready, 1)

            def positions(g, gb):
                past(pe, gmask_ready, g)
                past(pe, before_ready, g, 1)
                nc.tensor.matmul(slots_ps, tri[:, :], g_mask[gb][:, :, :], start=True, stop=False)
                nc.tensor.matmul(slots_ps, ones[:, :], g_before[gb][:, :].unsqueeze(1).to_broadcast([P, GROUP, NEXP]),
                                 start=False, stop=False)
                for j in range(GROUP - 1):
                    after = GROUP - 1 - j
                    nc.tensor.matmul(slots_ps[:, j + 1:, :], ones[:, :],
                                     g_mask[gb][:, j, :].unsqueeze(1).to_broadcast([P, after, NEXP]), start=False, stop=False)
                nc.tensor.matmul(slots_ps, ones[0:1, :], ebase[:, :].unsqueeze(1).to_broadcast([1, GROUP, NEXP]),
                                 start=False, stop=True).then_inc(pos_ready, 1)

            def step(i, u, q):
                if live(i, 6):
                    transpose_a(i - 6, (u - 6) % UNROLL)
                if live(i, 8):
                    transpose_x2(i - 8, (u - 8) % UNROLL)
                if u % GROUP == 1 and group_live(q):
                    positions(q - 3, (u // GROUP - 3) % 2)
                if live(i, 2):
                    project(i - 2, (u - 2) % UNROLL)
                if live(i, 6):
                    out_project(i - 6, (u - 6) % UNROLL)
                if live(i, 8):
                    gate(i - 8, (u - 8) % UNROLL, q)
                if live(i, 4):
                    sum_heads(i - 4, (u - 4) % UNROLL)
                if live(i, 1):
                    transpose_x(i - 1, (u - 1) % UNROLL)

            run_tiles(pe, step)

            pe.wait_ge(slot8_ready, NT // GROUP)
            pe.wait_ge(x2T_copied, NT)

            def take_in(n, b):
                pe.wait_ge(xe_loaded[b], (n - b) * 8 + 16)
                for k in range(2):
                    past(pe, x_lo_ready, n * 2 + k, 2)
                    for q in range(CB):
                        last = nc.tensor.transpose(p2_xT[k][:, q, :], xe[b][:, q, k * P:(k + 1) * P], ident[:, :])
                    last.then_inc(xe_transposed, 1)

            def first_layer(n, b, j, q, wb):
                past(pe, gated, n * NHT + j, 2)
                for half in range(2):
                    cols = slice(half * FF + j * P, half * FF + (j + 1) * P)
                    parts = [(w, x, k) for w, x in ((w1_lo, x_hi), (w1_hi, x_lo), (w1_hi, x_hi)) for k in range(2)]
                    for i, (w, x, k) in enumerate(parts):
                        last = nc.tensor.matmul(p2_h[q][half][:, :, :].rearrange("p b q -> p (b q)"), w[wb][:, k, cols],
                                                x[b][:, k, :], start=(i == 0), stop=(i == len(parts) - 1))
                last.then_inc(h_done, 1)

            def second_layer(n, b, wb):
                for k in range(CB):
                    if k % 2 == 0:
                        past(pe, y_scaled, n * CB + k + 1, CB)
                    parts = [(h, w, j) for h, w in ((h_lo, w2_hi), (h_hi, w2_lo), (h_hi, w2_hi)) for j in range(NHT)]
                    for i, (h, w, j) in enumerate(parts):
                        last = nc.tensor.matmul(p2_y[k // 2][:, k % 2, :], h[b][:, j, k * P:(k + 1) * P], w[wb][:, j, :],
                                                start=(i == 0), stop=(i == len(parts) - 1))
                    if k % 2 == 1:
                        last.then_inc(y_done, 1)

            def chunk_step(m, v, turn):
                b0, b1, b2 = v % 2, (v - 1) % 2, (v - 2) % 2
                wb1, wb2 = ((v - 1) // NCH) % 2, ((v - 2) // NCH) % 2
                for j in range(NHT):
                    if chunk_live(m, 1):
                        if j == 0:
                            pe.wait_ge(x_hi_ready, (m - 1) * 2 + 2)
                            pe.wait_ge(x_lo_ready, (m - 1) * 2 + 2)
                            past(pe, w_lo_ready, expert_of(v, turn, 1) * 2)
                        first_layer(m - 1, b1, j, (b1 * NHT + j) % 2, wb1)
                    if j == 0 and chunk_live(m, 0):
                        take_in(m, b0)
                    if j == second_layer_after(m) and chunk_live(m, 2):
                        past(pe, h_lo_ready, (m - 2) * NHT + NHT - 1)
                        past(pe, w_lo_ready, expert_of(v, turn, 2) * 2 + 1)
                        second_layer(m - 2, b2, wb2)

            run_chunks(pe, chunk_step)

        @block.vector
        def _(dve):
            dve.wait_ge(consts, 1)

            def lambda_terms():
                dve.wait_ge(w_loaded, W_LOADS)
                nc.vector.tensor_tensor(lam_prod[:, :, :], lam_in[:, :, 0, :], lam_in[:, :, 1, :], ALU.mult).then_inc(lam_chain, 1)
                dve.wait_ge(lam_chain, 1)
                nc.vector.tensor_reduce(lam_sum[:, :], lam_prod[:, :, :], AX_X, ALU.add).then_inc(lam_chain, 1)
                nc.vector.tensor_scalar(lnwb_s[:, 0:1], lnwb[:, 0:1], (1.0 - LAMBDA_INIT) * math.sqrt(DV) * RMS_SCALE, None, ALU.mult).then_inc(lam_ready, 1)
                nc.vector.tensor_scalar(lnwb_s[:, 1:2], lnwb[:, 1:2], 1.0 - LAMBDA_INIT, None, ALU.mult).then_inc(lam_ready, 1)
                dve.wait_ge(lam_ready, 3)
                nc.vector.tensor_tensor(neg_lam[:, :], lam_exp[:, 1:2], lam_exp[:, 0:1], ALU.subtract).then_inc(lam_chain, 1)
                dve.wait_ge(lam_chain, 3)
                nc.vector.tensor_scalar(neg_lam[:, :], neg_lam[:, :], LAMBDA_INIT, None, ALU.subtract).then_inc(lam_chain, 1)
                dve.wait_ge(lam_chain, 4)
                dve.wait_ge(consts, 2)

            arrive = {0: 0, 2: 1, 6: 2, 14: 3}

            def attention_added(t, b):
                past(dve, wo_done, t)
                nc.vector.tensor_tensor(x_tile(t), bank_wo[:, 0, :], x_tile(t), ALU.add).then_inc(x1_ready, 1)

            def score_products(t, b):
                past(dve, k_copied, t)
                past(dve, scores_ready, t, 1)
                q4 = bank_qk[b][:, 0, :].rearrange("p (n f) -> p n f", n=H).unsqueeze(2).to_broadcast([P, H, H, DV])
                k4 = k_sb[b][:, :].rearrange("p (m f) -> p m f", m=H).unsqueeze(1).to_broadcast([P, H, H, DV])
                nc.vector.tensor_tensor(qk_prod[:, :].rearrange("p (n m f) -> p n m f", n=H, m=H), q4, k4, ALU.mult).then_inc(qk_multiplied, 1)

            def score_sums(t, b):
                past(dve, qk_multiplied, t)
                nc.vector.tensor_reduce(s_raw[b][:, :, :, :].rearrange("p n m c -> p (n m c)"),
                                        qk_prod[:, :].rearrange("p (s d) -> p s d", d=D), AX_X, ALU.add).then_inc(scores_ready, 1)

            def score_max(t, b):
                past(dve, scores_ready, t)
                nc.vector.tensor_reduce(s_max[b][:, :, :], s_raw[b][:, :, :, :].rearrange("p n m c -> p n c m"),
                                        AX_X, ALU.max).then_inc(smax_ready, 1)

            def score_subtract(t, b):
                past(dve, smax_ready, t)
                past(dve, exp_done, t, 2)
                nc.vector.tensor_tensor(s_sub[b][:, :, :, :].rearrange("p c n m -> p n m c"), s_raw[b][:, :, :, :],
                                        s_max[b][:, :, :].unsqueeze(2).to_broadcast([P, H, H, 2]), ALU.subtract).then_inc(ssub_ready, 1)

            def prob_sum(t, b):
                past(dve, exp_done, t)
                nc.vector.tensor_reduce(p_sum[b][:, :], probs[b][:, :, :, :].rearrange("p c n m -> p (c n) m"),
                                        AX_X, ALU.add).then_inc(psum_ready, 1)

            def prob_reciprocal(t, b):
                past(dve, psum_ready, t)
                nc.vector.reciprocal(p_rec[b][:, :], p_sum[b][:, :]).then_inc(prec_ready, 1)

            def prob_normalise(t, b):
                past(dve, prec_ready, t)
                nc.vector.tensor_tensor(p_norm[b][:, :, :, :].rearrange("p c n m -> p (c n) m"),
                                        probs[b][:, :, :, :].rearrange("p c n m -> p (c n) m"),
                                        p_rec[b][:, :].unsqueeze(2).to_broadcast([P, 2 * H, H]), ALU.mult).then_inc(pnorm_ready, 1)

            def prob_difference(t, b):
                past(dve, pnorm_ready, t)
                past(dve, products_ready, t, 2)
                nc.vector.scalar_tensor_tensor(out=w_att[b][:, :, :].rearrange("p n m -> p (n m)"),
                                               in0=p_norm[b][:, 1, :, :].rearrange("p n m -> p (n m)"), scalar=neg_lam[:, :],
                                               in1=p_norm[b][:, 0, :, :].rearrange("p n m -> p (n m)"),
                                               op0=ALU.mult, op1=ALU.add).then_inc(w_ready, 1)

            def mean_terms(i, u):
                past(dve, rstd_ready, i)
                if live(i, 3):
                    past(dve, xn_ready, i - 3)
                if live(i, 9):
                    past(dve, xn2_ready, i - 9)
                nc.vector.scalar_tensor_tensor(out=neg_mr[u][:, :], in0=stat[u][:, H:H + 2, 0], scalar=-1.0,
                                               in1=rstd[u][:, H:H + 2], op0=ALU.mult, op1=ALU.mult).then_inc(neg_mr_ready, 1)

            def gate_max(g, gb, i):
                past(dve, logits_ready, i - 9)
                nc.vector.tensor_reduce(g_max[gb][:, :], logits, AX_X, ALU.max).then_inc(gmax_ready, 1)

            def gate_subtract(g, gb):
                past(dve, gmax_ready, g)
                nc.vector.tensor_tensor(g_sub[gb][:, :, :], logits, g_max[gb][:, :].unsqueeze(2).to_broadcast([P, GROUP, NEXP]),
                                        ALU.subtract).then_inc(gsub_ready, 1)

            def gate_top(g, gb):
                past(dve, gexp_done, g)
                nc.vector.tensor_reduce(g_sum[gb][:, :], g_exp[gb][:, :, :], AX_X, ALU.add).then_inc(gsum_ready, 1)
                for j in range(GROUP):
                    last = nc.vector.max(g_top[gb][:, j, :], g_exp[gb][:, j, :])
                last.then_inc(gtop_ready, 1)

            def gate_indices(g, gb):
                past(dve, gsum_ready, g)
                past(dve, gtop_ready, g)
                nc.vector.reciprocal(g_rec[gb][:, :], g_sum[gb][:, :]).then_inc(grec_ready, 1)
                for j in range(GROUP):
                    last = nc.vector.max_index(g_idx[gb][:, j, :], g_top[gb][:, j, :], g_exp[gb][:, j, :])
                last.then_inc(gidx_ready, 1)

            def row_weights(g, gb):
                past(dve, grec_ready, g)
                nc.vector.tensor_tensor(rows[:, gb * GROUP:(gb + 1) * GROUP, COL_W:COL_W + 2], g_top[gb][:, :, 0:2],
                                        g_rec[gb][:, :].unsqueeze(2).to_broadcast([P, GROUP, 2]), ALU.mult).then_inc(gweights_ready, 1)

            def row_experts(g, gb):
                past(dve, gidx_ready, g)
                nc.vector.tensor_copy(rows[:, gb * GROUP:(gb + 1) * GROUP, COL_EXP:COL_EXP + 2],
                                      g_idx[gb][:, :, 0:2]).then_inc(gexperts_ready, 1)

            def row_tokens(g, gb, i):
                t0 = i - 12
                src = tok_all[:, t0:t0 + GROUP] if isinstance(i, int) else tok_all[:, bass.ds(t0, GROUP)]
                nc.vector.tensor_copy(rows[:, gb * GROUP:(gb + 1) * GROUP, COL_TOK], src).then_inc(gtokens_ready, 1)

            def expert_hot(g, gb):
                past(dve, gexperts_ready, g)
                nc.vector.tensor_tensor(
                    g_hot[gb][:, :, :, :],
                    rows[:, gb * GROUP:(gb + 1) * GROUP, COL_EXP:COL_EXP + 2].unsqueeze(3).to_broadcast([P, GROUP, 2, NEXP]),
                    eiota[:, :].unsqueeze(1).unsqueeze(1).to_broadcast([P, GROUP, 2, NEXP]), ALU.is_equal).then_inc(ghot_ready, 1)

            def expert_mask(g, gb):
                past(dve, ghot_ready, g)
                nc.vector.tensor_tensor(g_mask[gb][:, :, :], g_hot[gb][:, :, 0, :], g_hot[gb][:, :, 1, :], ALU.add).then_inc(gmask_ready, 1)

            def expert_count(g, gb):
                past(dve, gmask_ready, g)
                nc.vector.tensor_reduce(g_count[gb][:, :], g_mask[gb][:, :, :].rearrange("p j e -> p e j"), AX_X, ALU.add).then_inc(gcount_ready, 1)

            def expert_before(g, gb):
                past(dve, gcount_ready, g)
                past(dve, pos_ready, g, 1)
                nc.vector.tensor_tensor(g_before[gb + 1][:, :], g_before[gb][:, :], g_count[gb][:, :], ALU.add).then_inc(before_ready, 1)

            def slot_over(g, gb):
                past(dve, pos_ready, g)
                nc.vector.tensor_tensor(g_over[gb][:, :, :], slots_ps, elimit[:, :].unsqueeze(1).to_broadcast([P, GROUP, NEXP]),
                                        ALU.is_ge).then_inc(over_ready, 1)

            def slot_pushed(g, gb):
                past(dve, over_ready, g)
                nc.vector.scalar_tensor_tensor(out=g_slot8[gb][:, :, :], in0=g_over[gb][:, :, :], scalar=OUT_OF_TABLE,
                                               in1=slots_ps, op0=ALU.mult, op1=ALU.add).then_inc(slot8_ready, 1)

            def slot_select(g, gb):
                past(dve, slot8_ready, g)
                nc.vector.tensor_tensor(g_sel[gb][:, :, :, :], g_hot[gb][:, :, :, :],
                                        g_slot8[gb][:, :, :].unsqueeze(2).to_broadcast([P, GROUP, 2, NEXP]), ALU.mult).then_inc(sel_ready, 1)

            def slot_sum(g, gb):
                past(dve, sel_ready, g)
                nc.vector.tensor_reduce(g_slotf[gb][:, :, :], g_sel[gb][:, :, :, :], AX_X, ALU.add).then_inc(slotf_ready, 1)

            def slot_integer(g, gb):
                past(dve, slotf_ready, g)
                nc.vector.tensor_copy(g_slot[gb][:, :, :], g_slotf[gb][:, :, :]).then_inc(slot_ready, 1)

            def step(i, u, q):
                routes = u % GROUP == 0 and group_live(q)
                slots = u % GROUP == 1 and group_live(q)
                g, gb = q - 3, (u // GROUP - 3) % 2
                b3 = (u - 3) % UNROLL
                slots_at_once = slots and not live(i, 3)
                slots_in_turns = slots and live(i, 3)
                if isinstance(i, int) and i == 2:
                    lambda_terms()
                if routes:
                    gate_max(g, gb, i)
                if live(i, 7):
                    past(dve, ln2_stats, i - 7)
                if live(i, 3):
                    score_products(i - 3, b3)
                if routes:
                    gate_subtract(g, gb)
                if slots:
                    slot_over(g, gb)
                if live(i, 7):
                    nc.vector.bn_aggr(stat[u][:, H + 1, :], bn2[u][:, :]).then_inc(ln2_aggr, 1)
                if live(i, 3):
                    score_sums(i - 3, b3)
                if slots_at_once:
                    slot_pushed(g, gb)
                    slot_select(g, gb)
                    slot_sum(g, gb)
                    slot_integer(g, gb)
                if slots_in_turns:
                    slot_pushed(g, gb)
                if routes:
                    gate_top(g, gb)
                if live(i, 3):
                    score_max(i - 3, b3)
                if slots_in_turns:
                    slot_select(g, gb)
                if roots_live(i):
                    mean_terms(i, u)
                if live(i, 3):
                    score_subtract(i - 3, b3)
                if slots_in_turns:
                    slot_sum(g, gb)
                if live(i, 0):
                    if isinstance(i, int) and i in arrive:
                        dve.wait_ge(x_loaded[arrive[i]], 16)
                    nc.vector.bn_stats(bn1[u][:, :], x_tile(i)).then_inc(ln1_stats, 1)
                if routes:
                    gate_indices(g, gb)
                if live(i, 6):
                    attention_added(i - 6, (u - 6) % UNROLL)
                if slots_in_turns:
                    slot_integer(g, gb)
                if routes:
                    row_weights(g, gb)
                    row_experts(g, gb)
                    row_tokens(g, gb, i)
                if live(i, 6):
                    past(dve, x1_ready, i - 6)
                if live(i, 3):
                    prob_sum(i - 3, b3)
                if routes:
                    expert_hot(g, gb)
                if live(i, 6):
                    nc.vector.bn_stats(bn2[(u + 1) % UNROLL][:, :], x_tile(i - 6)).then_inc(ln2_stats, 1)
                if live(i, 0):
                    past(dve, ln1_stats, i)
                if live(i, 3):
                    prob_reciprocal(i - 3, b3)
                if routes:
                    expert_mask(g, gb)
                if live(i, 0):
                    nc.vector.bn_aggr(stat[(u + 1) % UNROLL][:, H, :], bn1[u][:, :]).then_inc(ln1_aggr, 1)
                if live(i, 3):
                    prob_normalise(i - 3, b3)
                if routes:
                    expert_count(g, gb)
                if live(i, 3):
                    prob_difference(i - 3, b3)
                if routes:
                    expert_before(g, gb)

            run_tiles(dve, step)

            def slot_terms(n, b, e):
                dve.wait_ge(xe_loaded[b], (n - b) * 8 + 16)
                number = eiota[:, e:e + 1] if isinstance(e, int) else eiota[:, bass.ds(e, 1)]
                nc.vector.tensor_scalar(e_hit[b][:, :, :], xe[b][:, :, COL_EXP:COL_EXP + 2], number, None, ALU.is_equal).then_inc(hit_ready, 1)
                past(dve, hit_ready, n)
                nc.vector.tensor_tensor(e_w2[b][:, :, :], e_hit[b][:, :, :], xe[b][:, :, COL_W:COL_W + 2], ALU.mult).then_inc(wsel_ready, 1)
                past(dve, wsel_ready, n)
                past(dve, y_scaled, n, 2, CB)
                nc.vector.tensor_reduce(e_w[b][:, :], e_w2[b][:, :, :], AX_X, ALU.add).then_inc(wts_ready, 1)
                if not isinstance(n, int) or n >= 2:
                    dve.wait_ge(y_added[b], (n - b) * (8 * CB))
                nc.vector.tensor_copy(e_tok[b][:, :], xe[b][:, :, COL_TOK]).then_inc(toks_ready, 1)

            def input_low(n, b):
                for k in range(2):
                    past(dve, x_hi_ready, n * 2 + k)
                    nc.vector.tensor_tensor(x_lo[b][:, k, :], p2_xT[k][:, :, :].rearrange("p b q -> p (b q)"),
                                            x_hi[b][:, k, :], ALU.subtract).then_inc(x_lo_ready, 1)

            def gate_hidden(n, j, q):
                past(dve, silu_done, n * NHT + j)
                past(dve, h_hi_ready, n * NHT + j, 2)
                nc.vector.tensor_tensor(hidden[q][:, :], silu[q][:, :], p2_h[q][1][:, :, :].rearrange("p b q -> p (b q)"),
                                        ALU.mult).then_inc(gated, 1)

            def hidden_low(n, b, j, q):
                past(dve, h_hi_ready, n * NHT + j)
                nc.vector.tensor_tensor(h_lo[b][:, j, :], hidden[q][:, :], h_hi[b][:, j, :], ALU.subtract).then_inc(h_lo_ready, 1)

            def chunk_step(m, v, turn):
                b0, b1 = v % 2, (v - 1) % 2
                for j in range(NHT):
                    q = (b1 * NHT + j) % 2
                    if chunk_live(m, 1):
                        gate_hidden(m - 1, j, q)
                    if j == 0 and chunk_live(m, 0):
                        input_low(m, b0)
                    if chunk_live(m, 1):
                        hidden_low(m - 1, b1, j, q)
                if chunk_live(m, 0):
                    slot_terms(m, b0, expert_of(v, turn, 0))

            dve.wait_ge(x1_stored, 16 * (NT // 8))
            run_chunks(dve, chunk_step)


_INS = ['L0_attn_x', 'L0_attn_Wq', 'L0_attn_Wk', 'L0_attn_Wv', 'L0_attn_Wo', 'L0_attn_lambda_q1', 'L0_attn_lambda_k1',
        'L0_attn_lambda_q2', 'L0_attn_lambda_k2', 'L0_attn_ln_w', 'L0_attn_ln_b', 'L0_ffn_w_gate', 'L0_ffn_c_fc',
        'L0_ffn_c_proj']


def kernel(**inputs):
    import numpy as _np
    import concourse.bacc as _bacc
    from concourse import mybir as _mybir
    from concourse.bass_utils import run_bass_kernel_spmd as _run

    nc = _bacc.Bacc("TRN2", target_bir_lowering=False, num_devices=1)
    arrays, args = {}, []
    for name in _INS:
        a = _np.ascontiguousarray(inputs[name])
        arrays[f"in_{name}_dram"] = a
        args.append(nc.dram_tensor(f"in_{name}_dram", a.shape, _mybir.dt.from_np(a.dtype), kind="ExternalInput").ap())
    b, s, e = inputs["L0_attn_x"].shape
    args.append(nc.dram_tensor("out_0_dram", (b * s + CAP, e), _mybir.dt.float32, kind="ExternalOutput").ap())
    build_block(nc, *args)
    r = _run(nc, [arrays], core_ids=[0])
    return r.results[0]["out_0_dram"][:b * s].reshape(b, s, e)
```
